# Optimizing a Trainium2 kernel written in Bass

```python
import numpy as np
import jax
import jax.numpy as jnp

def _softmax(x, axis=-1):
    return jax.nn.softmax(x, axis=axis)

def _gelu(x):
    return jax.nn.gelu(x, approximate=True)

def _silu(x):
    return jax.nn.silu(x)

def _sigmoid(x):
    return jax.nn.sigmoid(x)

def _layernorm(x, axis=-1, eps=1e-05):
    m = jnp.mean(x, axis=axis, keepdims=True)
    v = jnp.var(x, axis=axis, keepdims=True)
    return (x - m) / jnp.sqrt(v + eps)

def _scatter_add(tgt, idx, src, axis=0):
    return tgt.at[idx].add(src)

def _segment_sum(src, seg, n):
    return jax.ops.segment_sum(src, seg, n)
kernel_name = 'mk_recurrent_d1_jaxref_r8_89405d'

def setup_inputs(seed: int=0):
    np.random.seed(seed)
    _w = jnp.asarray

    def _L0_attn_setup():
        import jax, jax.numpy as jnp
        import numpy as np
        D = 128
        H = 16
        DH = D // H
        key = jax.random.key(seed)
        ks = jax.random.split(key, 7)
        s = 0.02
        return {'z': jax.random.normal(ks[0], (8, 128, D), dtype=jnp.float32), 'ln_w': jnp.ones((D,), dtype=jnp.float32), 'ln_b': jnp.zeros((D,), dtype=jnp.float32), 'W_qkv': jax.random.normal(ks[1], (D, 3 * D), dtype=jnp.float32) * s, 'b_qkv': jnp.zeros((3 * D,), dtype=jnp.float32), 'W_proj': jax.random.normal(ks[2], (D, D), dtype=jnp.float32) * s, 'b_proj': jnp.zeros((D,), dtype=jnp.float32)}
    _L0_attn_in = _L0_attn_setup()

    def _L0_ffn_setup():
        import jax, jax.numpy as jnp
        import numpy as np
        from jax import lax
        D = 128
        H = 512
        E = 8
        TOPK = 2
        key = jax.random.key(seed)
        ks = jax.random.split(key, 7)
        s = 0.02
        return {'x': jax.random.normal(ks[0], (2, 256, D), dtype=jnp.float32), 'W1': jax.random.normal(ks[1], (E, D, H), dtype=jnp.float32) * s, 'b1': jnp.zeros((E, H), dtype=jnp.float32), 'W2': jax.random.normal(ks[2], (E, H, D), dtype=jnp.float32) * s, 'b2': jnp.zeros((E, D), dtype=jnp.float32), 'Wr': jax.random.normal(ks[3], (D, E), dtype=jnp.float32) * s, 'br': jnp.zeros((E,), dtype=jnp.float32)}
    _L0_ffn_in = _L0_ffn_setup()
    _d = {'L0_attn_z': _L0_attn_in['z'], 'L0_attn_ln_w': _L0_attn_in['ln_w'], 'L0_attn_ln_b': _L0_attn_in['ln_b'], 'L0_attn_W_qkv': _L0_attn_in['W_qkv'], 'L0_attn_b_qkv': _L0_attn_in['b_qkv'], 'L0_attn_W_proj': _L0_attn_in['W_proj'], 'L0_attn_b_proj': _L0_attn_in['b_proj'], 'L0_ffn_W1': _L0_ffn_in['W1'], 'L0_ffn_b1': _L0_ffn_in['b1'], 'L0_ffn_W2': _L0_ffn_in['W2'], 'L0_ffn_b2': _L0_ffn_in['b2'], 'L0_ffn_Wr': _L0_ffn_in['Wr'], 'L0_ffn_br': _L0_ffn_in['br']}
    _x0 = _d['L0_attn_z']
    _d['L0_attn_z'] = jax.random.normal(jax.random.fold_in(jax.random.key(seed), 1), (4, 1024, 128), dtype=_x0.dtype)
    del _x0
    return _d

def reference(L0_attn_z, L0_attn_ln_w, L0_attn_ln_b, L0_attn_W_qkv, L0_attn_b_qkv, L0_attn_W_proj, L0_attn_b_proj, L0_ffn_W1, L0_ffn_b1, L0_ffn_W2, L0_ffn_b2, L0_ffn_Wr, L0_ffn_br):

    def _L0_attn_ref(z, ln_w, ln_b, W_qkv, b_qkv, W_proj, b_proj):
        import jax, jax.numpy as jnp
        import numpy as np
        D = 128
        H = 16
        DH = D // H
        b, n, d = z.shape
        mu = jnp.mean(z, axis=-1, keepdims=True)
        var = jnp.var(z, axis=-1, keepdims=True)
        zn = (z - mu) / jnp.sqrt(var + 1e-05) * ln_w + ln_b
        qkv = (zn @ W_qkv + b_qkv).reshape(b, n, 3, H, DH)
        q = qkv[:, :, 0].transpose(0, 2, 1, 3)
        k = qkv[:, :, 1].transpose(0, 2, 1, 3)
        v = qkv[:, :, 2].transpose(0, 2, 1, 3)
        scale = 1.0 / jnp.sqrt(jnp.asarray(DH, dtype=z.dtype))
        scores = jnp.einsum('bhqd,bhkd->bhqk', q, k) * scale
        attn = jax.nn.softmax(scores, axis=-1)
        msa = jnp.einsum('bhqk,bhkd->bhqd', attn, v)
        msa_cat = msa.transpose(0, 2, 1, 3).reshape(b, n, d)
        out = msa_cat @ W_proj + b_proj
        return z + out

    def _L0_ffn_ref(x, W1, b1, W2, b2, Wr, br):
        import jax, jax.numpy as jnp
        import numpy as np
        from jax import lax
        D = 128
        H = 512
        E = 8
        TOPK = 2
        B, S, _ = x.shape
        xf = x.reshape(-1, D)
        logits = xf @ Wr + br
        topv, _ = lax.top_k(logits, TOPK)
        thresh = topv[:, TOPK - 1:TOPK]
        masked = jnp.where(logits >= thresh, logits, -jnp.inf)
        weights = jax.nn.softmax(masked, axis=-1)
        h = jax.nn.gelu(jnp.einsum('td,edh->eth', xf, W1) + b1[:, None, :], approximate=False)
        expert_out = jnp.einsum('eth,ehd->etd', h, W2) + b2[:, None, :]
        out = jnp.einsum('etd,te->td', expert_out, weights)
        return out.reshape(B, S, D)
    x = L0_attn_z
    xn = _layernorm(x, axis=-1)
    s = _L0_attn_ref(xn, L0_attn_ln_w, L0_attn_ln_b, L0_attn_W_qkv, L0_attn_b_qkv, L0_attn_W_proj, L0_attn_b_proj)
    g = _silu(_L0_ffn_ref(xn, L0_ffn_W1, L0_ffn_b1, L0_ffn_W2, L0_ffn_b2, L0_ffn_Wr, L0_ffn_br))
    x = x + s * g
    return x

_drawn_inputs = setup_inputs


def setup_inputs(seed=0):
    import zlib

    import numpy as np

    out = dict(_drawn_inputs(seed))
    spreads = {'L0_attn_ln_w': (1.0, 0.6),
     'L0_attn_ln_b': (0.0, 0.8),
     'L0_attn_b_qkv': (0.0, 0.8),
     'L0_attn_b_proj': (0.0, 0.8),
     'L0_ffn_b1': (0.0, 0.8),
     'L0_ffn_b2': (0.0, 0.1),
     'L0_ffn_br': (0.0, 0.1)}
    factors = {'L0_attn_W_qkv': 8.0, 'L0_attn_W_proj': 8.0, 'L0_ffn_W1': 2.961, 'L0_ffn_W2': 2.671}
    for name, (base, spread) in spreads.items():
        noise = np.random.default_rng([zlib.crc32(name.encode()), seed]).standard_normal(out[name].shape)
        drawn = base * np.exp(spread * noise) if base else spread * noise
        out[name] = jnp.asarray(drawn.astype(out[name].dtype))
    for name, factor in factors.items():
        out[name] = (out[name] * factor).astype(out[name].dtype)
    return out
```

```python
from contextlib import ExitStack

import concourse.bass as bass
from concourse import mybir

ALU = mybir.AluOpType
ACT = mybir.ActivationFunctionType
AX = mybir.AxisListType
F32 = mybir.dt.float32
F32R = mybir.dt.float32r
BF16 = mybir.dt.bfloat16
I32 = mybir.dt.int32

P = 128
TG = 512
TT = TG // P
PARTS = 3
QROWS = 96
SROWS = QROWS + PARTS
VC = 32
EPS = 1e-5
RSQRT_GUESS = 0x5F3759DF
NEWTON = 3


class Chain:

    def __init__(self, eng, sem):
        self.eng, self.sem, self.n = eng, sem, 0

    def mark(self, ins):
        self.n += 1
        ins.then_inc(self.sem, 1)

    def sync(self):
        self.eng.wait_ge(self.sem, self.n)

    def end(self):
        self.sync()
        self.eng.sem_inc(self.sem, -self.n)
        self.n = 0


def run_slots(n, *plans):
    for s in range(n):
        for plan in plans:
            for step in plan.get(s, []):
                step()


def attention_and_experts(nc, x, ln_w, ln_b, w_qkv, b_qkv, w_proj, b_proj, w1, b1, w2, b2, w_r, b_r, out):
    B, N, D = x.shape
    E, _, HID = w1.shape
    H = 16
    DH = D // H
    SCALE = float(DH) ** -0.5
    NG = B * N // TG
    HC = HID // P
    HT = E * HC
    KT = N // P
    NT = N // P
    NHEAD = B * H
    HB = 4
    NIT = NHEAD // HB
    NSLOT = HT + 5
    assert D == P and N % TG == 0 and N // TG == 2 and HID % P == 0

    x_g = x.rearrange("b (g t p) d -> (b g) p t d", p=P, t=TT)
    out_g = out.rearrange("b (g t p) d -> (b g) p t d", p=P, t=TT)

    q_dram = nc.dram_tensor("q_parts_dram", (B, D, PARTS, N), BF16, kind="Internal").ap()
    k_dram = nc.dram_tensor("k_parts_dram", (PARTS, B, D, PARTS, N), BF16, kind="Internal").ap()
    w_dram = nc.dram_tensor("expert_w_dram", (NG, TT, E, P), F32, kind="Internal").ap()
    m_dram = nc.dram_tensor("neg_max_dram", (HB, PARTS * NT, P), BF16, kind="Internal").ap()
    q_rows = q_dram.rearrange("b r i t -> (b r i) t")
    k_rows = k_dram.rearrange("j b r i t -> j (b r i) t")

    with ExitStack() as ctx:
        def sb(name, shape, dt=F32, c=ctx):
            return c.enter_context(nc.sbuf_tensor(name, shape, dt))

        def sem(name):
            return ctx.enter_context(nc.semaphore(name))

        xh = sb("xn_t_hi", [P, NG, TG], F32R)
        xl = sb("xn_t_lo", [P, NG, TG], F32R)
        ffn = sb("ffn_t", [P, NG, TG])
        v_sb = sb("v_sb", [P, B * KT, D])
        q_st = sb("q_stack", [P, HB, N], BF16)
        k_st = sb("k_stack", [P, HB, N], BF16)
        ident = sb("ident", [P, P])
        ident_b = sb("ident_b", [P, P], BF16)
        cols = sb("cols", [P, 64])
        wp_sb = sb("wp_sb", [P, D])
        zero8 = sb("zero8", [P, NT])

        ffn_ctx = ExitStack()
        fs = lambda name, shape, dt=F32: sb(name, shape, dt, ffn_ctx)
        w1h = fs("w1_hi", [P, E, HID], F32R)
        w1l = fs("w1_lo", [P, E, HID], F32R)
        w2h = fs("w2_hi", [P, E, HC * D], F32R)
        w2l = fs("w2_lo", [P, E, HC * D], F32R)
        wbc = fs("expert_w_bc", [P, E, TG])
        hh = fs("h_hi", [P, 4, TG], F32R)
        hl = fs("h_lo", [P, 4, TG], F32R)
        h32 = fs("h_full", [P, 2, TG])
        prod = fs("prod", [P, 2, TG])
        acc = fs("acc", [P, TG])
        rows = fs("rows", [48, P])
        xz = fs("xz", [P, TT, D])
        xnT = fs("xn_t", [P, TG])
        znT = fs("zn_t", [P, TG])
        qkf = fs("qk_full", [P, 2, TG])
        qkp = fs("qk_parts", [P, 2, PARTS, TG], BF16)
        wqkv_sb = fs("wqkv_sb", [P, 3 * D])
        wr_sb = fs("wr_sb", [P, E])
        bv_bc = fs("bv_bc", [P, D])
        br_bc = fs("br_bc", [P, E])
        st1 = fs("bn_parts", [P, TT, 6])
        mv = fs("mean_var", [P, TT, 2])
        nwt = fs("newton", [P, 4, TT])
        guess = fs("guess", [P, TT], I32)
        lg = fs("logits", [P, TT, E])
        top = fs("top8", [P, TT, 8])
        rt = fs("router", [P, 6, TT, E])
        rs = fs("router_sum", [P, 2, TT])
        wT = fs("w_t", [TT * E, P])
        ffn_ctx.close()
        w_raw = ffn

        att_ctx = ExitStack()
        ats = lambda name, shape, dt=F32: sb(name, shape, dt, att_ctx)
        p_sb = ats("p_ring", [P, 4, N])
        v_st = ats("v_stack", [P, HB, KT, VC])
        mx = ats("neg_max", [P, HB, NT])
        nm = ats("neg_max_rest", [P, HB, NT])
        nmp = ats("neg_max_parts", [P, HB, PARTS, NT], BF16)
        nmT = ats("neg_max_t", [PARTS * NT, HB, P], BF16)
        o_sb = ats("o_sb", [P, 2, TG])
        o9 = ats("o_sum", [P, 2, NT, DH + 1])
        rden = ats("rden", [P, 2, NT])
        msa = ats("msa", [P, B * NT, D])
        msaT = ats("msa_t", [P, 2, TG])
        y1 = ats("y1", [P, 2, TG])
        y2 = ats("y2", [P, 2, TG])
        x_out = ats("x_out", [P, 2, TT, D])
        att_ctx.close()

        psum = ctx.enter_context(nc.psum_tensor("psum", [P, 8 * TG], F32))
        bank = [psum[:, i * TG:(i + 1) * TG] for i in range(8)]
        wide_banks = [psum[:, (2 + 2 * i) * TG:(4 + 2 * i) * TG] for i in range(2)]
        b5, b6, b7 = bank[5], bank[6], bank[7]
        m_tr = b7[0:PARTS * NT, 0:P // 2].bitcast(BF16)

        C_B1, C_B2 = 0, HT
        C_LNW, C_LNB, C_BQ, C_BK, C_BP = (HT + E + i for i in range(5))
        NROW = HT + E + 5

        def col(i):
            return cols[:, i:i + 1]

        s = {}

        def S(name):
            if name not in s:
                s[name] = sem("s_" + name)
            return s[name]

        for name in ("const w_raw0 w_raw1 w_raw2 w_raw3 w_hi w_lo rows ident zeros cols_t cols x xn zn t1 t2 "
                     "xnT znT xh xl lg dlt th w wt wT w_st qp_st q k v qf kf r1 p1 qp vd "
                     "h hh h32 hl m2 stt acc gate dve pool "
                     "S P PV M R nmp mT mTc m_st m_ld0 m_ld1 m_ld2 m_ld3 st0 st1 st2 st3 vst oe ot os msa "
                     "adve apool tm tmc tp y ya yg tt ty rd tx0 tx1 out0 out1 vinit tdve").split():
            S(name)
        s_wbc = [sem(f"s_wbc{e}") for e in range(E)]

        def wait(eng, name, it, per, k):
            if isinstance(it, int):
                if it * per + k > 0:
                    eng.wait_ge(S(name), it * per + k)
            else:
                eng.wait_ge(S(name), it * per + k)

        def G(t, g):
            return t[:, g, :] if isinstance(g, int) else t[:, bass.ds(g, 1), :].rearrange("p a t -> p (a t)")

        block = ctx.enter_context(nc.Block())

        QP_ST = 6 * 16

        def sp_weight(sp, n):
            e, slot = n // 2, n % 4
            if n >= 4:
                sp.wait_ge(S("w_lo"), n - 3)
            dst = w_raw[:, 4 + slot, :]
            if n % 2 == 0:
                sp.dma_start(dst, w1[e, :, :]).then_inc(S(f"w_raw{slot}"), 16)
            else:
                sp.dma_start(dst.rearrange("p (c d) -> p c d", c=HC),
                             w2[e, :, :].rearrange("(c p) d -> p c d", p=P)).then_inc(S(f"w_raw{slot}"), 16)

        def sp_load_x(sp, g):
            def step():
                wait(sp, "t2", g, 1, 0)
                src = x_g[g] if isinstance(g, int) else x_g[bass.ds(g, 1)].rearrange("a p t d -> (a p) t d")
                sp.dma_start(xz[:, :, :], src).then_inc(S("x"), 16)
            return step

        def sp_pre(sp, g):
            b, half = (g // 2, g % 2)

            def store_w():
                wait(sp, "wT", g, 1, 1)
                dst = w_dram[g] if isinstance(g, int) else w_dram[bass.ds(g, 1)].rearrange("a t e p -> (a t) e p")
                sp.dma_start(dst.rearrange("t e p -> (t e) p"), wT[:, :]).then_inc(S("w_st"), 16)

            def cut(t, bb):
                return t[bb] if isinstance(bb, int) else t[bass.ds(bb, 1)].rearrange("a r i t -> (a r) i t")

            def store_q():
                wait(sp, "qp", g, 2, 1)
                sp.dma_start(cut(q_dram, b)[:, :, tok(half)], qkp[:, 0, :, :]).then_inc(S("qp_st"), 16)

            def store_k():
                wait(sp, "qp", g, 2, 2)
                for j in range(PARTS):
                    dst = cut(k_dram[j], b)[:, :, tok(half)]
                    sp.dma_start(dst[:, 0:PARTS - j, :], qkp[:, 1, j:PARTS, :]).then_inc(S("qp_st"), 16)
                    if j:
                        sp.dma_start(dst[:, PARTS - j:PARTS, :], qkp[:, 1, 0:j, :]).then_inc(S("qp_st"), 16)

            def tok(hf):
                return slice(hf * TG, (hf + 1) * TG) if isinstance(hf, int) else bass.ds(hf * TG, TG)

            return {25: [store_w], 28: [store_q], 30: [store_k]}

        def sp_wbc(sp, g, e):
            def step():
                if e == 0:
                    wait(sp, "w_st", g, 16, 16)
                wait(sp, "stt", g, E, e + 1 - E)
                src = w_dram[g, :, e, :] if isinstance(g, int) else \
                    w_dram[bass.ds(g, 1), :, e, :].rearrange("a t p -> (a t) p")
                sp.dma_start(wbc[:, e, :].rearrange("p (t c) -> p t c", t=TT), src.partition_broadcast(P))\
                    .then_inc(s_wbc[e], 16)
            return step

        def sp_stage(sp, n, u):
            r0 = n * (DH * PARTS)

            def rows_of(t):
                return t[r0:r0 + DH * PARTS, :] if isinstance(n, int) else t[bass.ds(r0, DH * PARTS), :]
            for j in range(PARTS):
                lo = j * DH * PARTS
                sp.dma_start(q_st[lo:lo + DH * PARTS, u, :], rows_of(q_rows)).then_inc(S(f"st{u}"), 16)
                sp.dma_start(k_st[lo:lo + DH * PARTS, u, :], rows_of(k_rows[j])).then_inc(S(f"st{u}"), 16)

        def sp_att(sp, it, last):
            for u in range(HB):
                m = u + 1
                if not (last and m >= HB):
                    slot, mit = m % HB, it + m // HB
                    wait(sp, "mTc", mit, HB, slot + 1)
                    sp.dma_start(m_dram[slot], nmT[:, slot, :]).then_inc(S("m_st"), 16)
                    wait(sp, "m_st", mit, HB * 16, (slot + 1) * 16)
                    sp.dma_start(q_st[QROWS:SROWS, slot, :],
                                 m_dram[slot].rearrange("(i t) c -> i (t c)", i=PARTS)).then_inc(S(f"m_ld{slot}"), 16)
                if not last:
                    wait(sp, "S", it, HB * 2 * KT, (u + 1) * 2 * KT)
                    sp_stage(sp, (it + 1) * HB + u, u)

        @block.sync
        def _(sp):
            sp_load_x(sp, 0)()
            for r0, r1, src in ((0, HT, b1.rearrange("e (c p) -> (e c) p", p=P)), (HT, HT + E, b2),
                                (C_LNW, C_LNW + 1, ln_w.rearrange("(a p) -> a p", a=1)),
                                (C_LNB, C_LNB + 1, ln_b.rearrange("(a p) -> a p", a=1)),
                                (C_BQ, C_BQ + 2, b_qkv[0:2 * D].rearrange("(a p) -> a p", p=P)),
                                (C_BP, C_BP + 1, b_proj.rearrange("(a p) -> a p", a=1))):
                sp.dma_start(rows[r0:r1, :], src).then_inc(S("rows"), 16)
            sp.dma_start(wqkv_sb[:, :], w_qkv).then_inc(S("const"), 16)
            sp.dma_start(wr_sb[:, :], w_r).then_inc(S("const"), 16)
            sp.dma_start(wp_sb[:, :], w_proj).then_inc(S("const"), 16)
            sp.dma_start(bv_bc[:, :], b_qkv[2 * D:3 * D].partition_broadcast(P)).then_inc(S("const"), 16)
            sp.dma_start(br_bc[:, :], b_r.partition_broadcast(P)).then_inc(S("const"), 16)
            for n in range(4):
                sp_weight(sp, n)
            pre = sp_pre(sp, 0)
            for k in sorted(pre):
                for f in pre[k]:
                    f()
            sp_load_x(sp, 1)()
            for e in range(E):
                sp_wbc(sp, 0, e)()
            for n in range(4, 2 * E):
                sp_weight(sp, n)

            def body(g):
                plan = sp_pre(sp, g + 1)
                run_slots(NSLOT, plan)
                for e in range(E):
                    sp_wbc(sp, g + 1, e)()

            body(0)
            sp_load_x(sp, 2)()
            with sp.Fori(1, NG - 2) as g:
                body(g)
                sp_load_x(sp, g + 2)()
            body(NG - 2)
            sp.wait_ge(S("zeros"), 4)
            sp.wait_ge(S("qp_st"), NG * QP_ST)
            for u in range(HB):
                sp_stage(sp, u, u)
            sp.wait_ge(S("mTc"), 1)
            sp.dma_start(m_dram[0], nmT[:, 0, :]).then_inc(S("m_st"), 16)
            sp.wait_ge(S("m_st"), 16)
            sp.dma_start(q_st[QROWS:SROWS, 0, :], m_dram[0].rearrange("(i t) c -> i (t c)", i=PARTS))\
                .then_inc(S("m_ld0"), 16)
            sp_att(sp, 0, False)
            with sp.Fori(1, NIT - 1) as it:
                sp_att(sp, it, False)
            sp_att(sp, NIT - 1, True)

            for g in range(NG):
                k = g % 2
                if g >= 2:
                    wait(sp, "ty", 0, 0, g - 1)
                    sp.dma_start(out_g[g - 2], x_out[:, k, :, :]).then_inc(S(f"out{k}"), 16)
                    wait(sp, f"out{k}", 0, 0, 16 * (g // 2))
                sp.dma_start(x_out[:, k, :, :], x_g[g]).then_inc(S(f"tx{k}"), 16)
            for g in (NG - 2, NG - 1):
                wait(sp, "ty", 0, 0, g + 1)
                sp.dma_start(out_g[g], x_out[:, g % 2, :, :]).then_inc(S(f"out{g % 2}"), 16)
            for k in (0, 1):
                sp.wait_ge(S(f"out{k}"), 16 * (NG // 2))
            sp.wait_ge(S("qp_st"), NG * QP_ST)
            sp.wait_ge(S("w_st"), NG * 16)
            sp.wait_ge(S("m_st"), NHEAD * 16)

        @block.gpsimd
        def _(pool):
            for n, t in enumerate((ident, ident_b)):
                pool.memset(t[:, :], 0.0).then_inc(S("pool"), 1)
                pool.wait_ge(S("pool"), n + 1)
                pool.affine_select(out=t[:, :], in_=t[:, :], compare_op=ALU.not_equal, fill=1.0, base=0,
                                   pattern=[[-1, P]], channel_multiplier=1).then_inc(S("ident"), 1)
            def weights_lo(n):
                e, slot = n // 2, n % 4
                hi, lo = ((w1h, w1l), (w2h, w2l))[n % 2]
                pool.wait_ge(S("w_hi"), n + 1)
                pool.tensor_tensor(lo[:, e, :], w_raw[:, 4 + slot, :], hi[:, e, :].bitcast(F32), ALU.subtract)\
                    .then_inc(S("w_lo"), 1)

            def pre(g):
                def rest(w):
                    def step():
                        wait(pool, ("qf", "kf")[w], g, 1, 1)
                        pool.tensor_tensor(qkf[:, w, :], qkf[:, w, :], qkp[:, w, 0, :], ALU.subtract)\
                            .then_inc(S("r1"), 1)
                    return step

                def third(w):
                    def step():
                        wait(pool, "p1", g, 2, w + 1)
                        pool.tensor_tensor(qkp[:, w, 2, :], qkf[:, w, :], qkp[:, w, 1, :], ALU.subtract)\
                            .then_inc(S("qp"), 1)
                    return step
                return {22: [rest(0)], 23: [rest(1)], 26: [third(0)], 27: [third(1)]}

            def experts(g):
                def add(e):
                    def step():
                        wait(pool, "stt", g, E, e + 1)
                        if e > 1:
                            wait(pool, "acc", g, E - 1, e - 1)
                        pool.tensor_tensor(acc[:, :], acc[:, :], prod[:, e % 2, :], ALU.add).then_inc(S("acc"), 1)
                    return step
                return {4 * e + 7: [add(e)] for e in range(1, E - 1)}

            for n in range(4):
                weights_lo(n)
            run_slots(NSLOT, pre(0))
            for n in range(4, 2 * E):
                weights_lo(n)
            run_slots(NSLOT, experts(0), pre(1))
            with pool.Fori(1, NG - 1) as g:
                run_slots(NSLOT, experts(g), pre(g + 1))
            run_slots(NSLOT, experts(NG - 1))

            pool.wait_ge(S("m2"), NG * HT)
            pool.memset(v_st[:, :, :, DH + 1:VC], 0.0).then_inc(S("vinit"), 1)
            pool.memset(v_st[:, :, :, DH:DH + 1], 1.0).then_inc(S("vinit"), 1)
            ch = Chain(pool, S("apool"))

            def stage_v(it, u):
                b, h = it // (H // HB), (it % (H // HB)) * HB + u
                wait(pool, "PV", it, HB * KT // 2, (u + 1 - HB) * KT // 2)
                if isinstance(b, int):
                    src = v_sb[:, b * KT:(b + 1) * KT, h * DH:(h + 1) * DH]
                else:
                    src = v_sb[:, bass.ds(b * KT, KT), bass.ds(h * DH, DH)]
                pool.tensor_copy(v_st[:, u, :, 0:DH], src).then_inc(S("vst"), 1)

            def neg_parts(it, u):
                wait(pool, "R", it, HB * NT, (u + 1) * NT)
                a, r = mx[:, u, :], nm[:, u, :]
                p = [nmp[:, u, i, :] for i in range(PARTS)]
                ch.mark(pool.tensor_tensor(p[0], a, zero8[:, :], ALU.add))
                ch.sync()
                ch.mark(pool.tensor_tensor(r, a, p[0], ALU.subtract))
                ch.sync()
                ch.mark(pool.tensor_copy(p[1], r))
                ch.end()
                pool.tensor_tensor(p[2], r, p[1], ALU.subtract).then_inc(S("nmp"), 1)

            def att(it, first, last):
                for u in range(HB):
                    if not (first and u == 0):
                        stage_v(it, u)
                    m = u + 2
                    if m < HB:
                        neg_parts(it, m)
                    elif not last:
                        neg_parts(it + 1, m - HB)

            pool.wait_ge(S("vd"), NG)
            stage_v(0, 0)
            for u in range(2):
                neg_parts(0, u)
            att(0, True, False)
            with pool.Fori(1, NIT - 1) as it:
                att(it, False, False)
            att(NIT - 1, False, True)

        @block.scalar
        def _(act):
            act.wait_ge(S("cols_t"), 1)
            act.activation(cols[:, 0:NROW], b7[:, 0:NROW], ACT.Copy).then_inc(S("cols"), 1)

            def weights_hi(n):
                e, slot = n // 2, n % 4
                hi = (w1h, w2h)[n % 2]
                act.wait_ge(S(f"w_raw{slot}"), 16 * (n // 4 + 1))
                act.activation(hi[:, e, :], w_raw[:, 4 + slot, :], ACT.Copy).then_inc(S("w_hi"), 1)

            def pre(g):
                def x_t():
                    wait(act, "t1", g, 1, 1)
                    wait(act, "xl", g, 1, 0)
                    wait(act, "lg", g, 1, 0)
                    act.activation(xnT[:, :], b5[:, :], ACT.Copy).then_inc(S("xnT"), 1)

                def z_t():
                    if isinstance(g, int) and g == 0:
                        act.wait_ge(S("cols"), 1)
                    wait(act, "t2", g, 1, 1)
                    wait(act, "v", g, 1, 0)
                    act.activation(znT[:, :], b6[:, :], ACT.Identity, scale=col(C_LNW), bias=col(C_LNB))\
                        .then_inc(S("znT"), 1)

                def qk(w):
                    def step():
                        wait(act, ("q", "k")[w], g, 1, 1)
                        wait(act, "qp_st", g, QP_ST, 0)
                        bk, bias = ((b5, C_BQ), (b6, C_BK))[w]
                        act.activation(qkp[:, w, 0, :], bk[:, :], ACT.Identity, bias=col(bias))
                        act.activation(qkf[:, w, :], bk[:, :], ACT.Identity, bias=col(bias))\
                            .then_inc(S(("qf", "kf")[w]), 1)
                    return step

                def tanh():
                    wait(act, "dlt", g, 1, 1)
                    act.activation(rt[:, 1, :, :], rt[:, 0, :, :], ACT.Tanh, scale=0.5).then_inc(S("th"), 1)

                def w_t():
                    wait(act, "wt", g, 1, 1)
                    wait(act, "w_st", g, 16, 0)
                    act.activation(wT[:, :], b7[0:TT * E, 0:P], ACT.Copy).then_inc(S("wT"), 1)
                return {11: [x_t], 16: [z_t], 18: [tanh], 20: [qk(0)], 21: [qk(1)], 24: [w_t]}

            def experts(g):
                def gelu(i):
                    def step():
                        wait(act, "h", g, HT, i + 1)
                        wait(act, "m2", g, HT, max(i - 3, 0) if i >= 4 else 0)
                        e, c = i // HC, i % HC
                        act.activation(hh[:, i % 4, :], bank[i % 2][:, :], ACT.Gelu, bias=col(C_B1 + i))\
                            .then_inc(S("hh"), 1)
                        wait(act, "hl", g, HT, max(i - 1, 0))
                        act.activation(h32[:, i % 2, :], bank[i % 2][:, :], ACT.Gelu, bias=col(C_B1 + i))\
                            .then_inc(S("h32"), 1)
                    return step
                return {i: [gelu(i)] for i in range(HT)}

            p0 = pre(0)
            for n in range(4):
                weights_hi(n)
            run_slots(NSLOT, p0)
            for n in range(4, 2 * E):
                weights_hi(n)
            run_slots(NSLOT, experts(0), pre(1))
            with act.Fori(1, NG - 1) as g:
                run_slots(NSLOT, experts(g), pre(g + 1))
            run_slots(NSLOT, experts(NG - 1))
            act.wait_ge(S("acc"), NG * (E - 1))
            act.activation(ffn[:, :, :], ffn[:, :, :], ACT.Silu).then_inc(S("gate"), 1)

            def neg_max_t(it, u):
                wait(act, "mT", it, HB, u + 1)
                act.activation(nmT[:, u, :], m_tr, ACT.Copy).then_inc(S("mTc"), 1)

            def o_copy(it, u):
                wait(act, "PV", it, HB * KT // 2, (u + 1) * KT // 2)
                wait(act, "ot", it, HB, u - 1)
                act.activation(o_sb[:, u % 2, :], b6[:, :], ACT.Copy).then_inc(S("oe"), 1)

            def att(it, first, last):
                for u in range(HB):
                    for kt in range(KT):
                        for a in range(2):
                            i = 2 * kt + a
                            wait(act, "S", it, HB * 2 * KT, u * 2 * KT + i + 1)
                            if a == 0 and kt % 2 == 0:
                                wait(act, "PV", it, HB * KT // 2, u * KT // 2 + kt // 2 - 1)
                            act.activation(p_sb[:, kt % 4, a * TG:(a + 1) * TG], bank[i % 2][:, :], ACT.Exp,
                                           scale=SCALE).then_inc(S("P"), 1)
                        if kt == 1:
                            if u:
                                o_copy(it, u - 1)
                            elif not first:
                                o_copy(it - 1, HB - 1)
                        if kt == 2:
                            m = u + 1
                            if m < HB:
                                neg_max_t(it, m)
                            elif not last:
                                neg_max_t(it + 1, 0)

            neg_max_t(0, 0)
            att(0, True, False)
            with act.Fori(1, NIT - 1) as it:
                att(it, False, False)
            att(NIT - 1, False, True)
            o_copy(NIT - 1, HB - 1)

            for g in range(NG):
                k = g % 2
                wait(act, "tm", 0, 0, g + 1)
                wait(act, "tp", 0, 0, g - 1)
                act.activation(msaT[:, k, :], bank[k][:, :], ACT.Copy).then_inc(S("tmc"), 1)

        @block.tensor
        def _(pe):
            pe.wait_ge(S("ident"), 2)
            pe.wait_ge(S("rows"), 6 * 16)
            pe.transpose(b7[:, 0:NROW], rows[0:NROW, :], ident[0:NROW, 0:NROW]).then_inc(S("cols_t"), 1)
            pe.wait_ge(S("const"), 5 * 16)

            def pre(g):
                def t1():
                    wait(pe, "xn", g, 1, 1)
                    wait(pe, "qf", g, 1, 0)
                    for t in range(TT):
                        m = pe.transpose(b5[:, t * P:(t + 1) * P], xz[:, t, :], ident[:, :])
                    m.then_inc(S("t1"), 1)

                def t2():
                    wait(pe, "zn", g, 1, 1)
                    wait(pe, "kf", g, 1, 0)
                    for t in range(TT):
                        m = pe.transpose(b6[:, t * P:(t + 1) * P], xz[:, t, :], ident[:, :])
                    m.then_inc(S("t2"), 1)

                def logits():
                    wait(pe, "xnT", g, 1, 1)
                    if isinstance(g, int) and g == 0:
                        pe.wait_ge(S("cols"), 1)
                    wait(pe, "vd", g, 1, 0)
                    for t in range(TT):
                        m = pe.matmul(b7[:, t * E:(t + 1) * E], xnT[:, t * P:(t + 1) * P], wr_sb[:, :],
                                      start=True, stop=True)
                    m.then_inc(S("lg"), 1)

                def qk():
                    wait(pe, "znT", g, 1, 1)
                    pe.matmul(b5[:, :], wqkv_sb[:, 0:D], znT[:, :], start=True, stop=True).then_inc(S("q"), 1)
                    pe.matmul(b6[:, :], wqkv_sb[:, D:2 * D], znT[:, :], start=True, stop=True).then_inc(S("k"), 1)

                def w_t():
                    wait(pe, "w", g, 1, 1)
                    pe.transpose(b7[0:TT * E, 0:P], rt[:, 5, :, :].rearrange("p t e -> p (t e)"), ident[:, :])\
                        .then_inc(S("wt"), 1)

                def v():
                    wait(pe, "wT", g, 1, 1)
                    for t in range(TT):
                        m = pe.matmul(b7[:, t * P:(t + 1) * P], znT[:, t * P:(t + 1) * P], wqkv_sb[:, 2 * D:3 * D],
                                      start=True, stop=True)
                    m.then_inc(S("v"), 1)
                return {9: [t1], 14: [logits], 15: [t2], 18: [qk], 22: [w_t], HT: [v]}

            def experts(g):
                def up(i):
                    def step():
                        if i == 0:
                            wait(pe, "xl", g, 1, 1)
                        if isinstance(g, int) and g == 0 and i % HC == 0:
                            pe.wait_ge(S("w_lo"), 2 * (i // HC) + 2)
                        wait(pe, "h32", g, HT, max(i - 1, 0))
                        e, c = i // HC, i % HC
                        o = bank[i % 2][:, :]
                        ws = slice(c * P, (c + 1) * P)
                        pe.matmul(o, w1h[:, e, ws], G(xh, g), start=True, stop=False)
                        pe.matmul(o, w1l[:, e, ws], G(xh, g), start=False, stop=False)
                        pe.matmul(o, w1h[:, e, ws], G(xl, g), start=False, stop=True).then_inc(S("h"), 1)
                    return step

                def down(i):
                    def step():
                        e, c = i // HC, i % HC
                        if c == 0:
                            wait(pe, "stt", g, E, max(e - 1, 0))
                        o = bank[2 + e % 2][:, :]
                        ws = slice(c * D, (c + 1) * D)
                        wait(pe, "hh", g, HT, i + 1)
                        pe.matmul(o, w2h[:, e, ws], hh[:, i % 4, :], start=(c == 0), stop=False)
                        pe.matmul(o, w2l[:, e, ws], hh[:, i % 4, :], start=False, stop=False)
                        wait(pe, "hl", g, HT, i + 1)
                        pe.matmul(o, w2h[:, e, ws], hl[:, i % 4, :], start=False, stop=(c == HC - 1))\
                            .then_inc(S("m2"), 1)
                    return step
                plan = {i: [up(i)] for i in range(HT)}
                for i in range(HT):
                    plan.setdefault(i + 2, []).append(down(i))
                return plan

            run_slots(NSLOT, pre(0))
            run_slots(NSLOT, pre(1), experts(0))
            with pe.Fori(1, NG - 1) as g:
                run_slots(NSLOT, pre(g + 1), experts(g))
            run_slots(NSLOT, experts(NG - 1))

            def max_scores(it, u, t, first=False):
                if t == 0:
                    wait(pe, f"st{u}", it, 96, 96)
                wait(pe, "R", it, HB * NT, u * NT + t - 1)
                for c in range(2):
                    m = pe.matmul(bank[2 + 2 * (t % 2) + c][:, :], q_st[0:QROWS, u, t * P:(t + 1) * P],
                                  k_st[0:QROWS, u, c * TG:(c + 1) * TG], start=True, stop=True)
                m.then_inc(S("M"), 1)

            def scores(it, u, i):
                kt, a = i // 2, i % 2
                wait(pe, "P", it, HB * 2 * KT, u * 2 * KT + i - 1)
                pe.matmul(bank[i % 2][:, :], k_st[0:SROWS, u, kt * P:(kt + 1) * P],
                          q_st[0:SROWS, u, a * TG:(a + 1) * TG], start=True, stop=True).then_inc(S("S"), 1)

            def pv(it, u, m):
                if m == 0:
                    wait(pe, "vst", it, HB, u + 1)
                    wait(pe, "oe", it, HB, u)
                wait(pe, "P", it, HB * 2 * KT, u * 2 * KT + 4 * m + 4)
                for g4 in range(4):
                    kt, a = 2 * m + g4 // 2, g4 % 2
                    mm = pe.matmul(b6[VC * g4:VC * (g4 + 1), :], v_st[:, u, kt, :],
                                   p_sb[:, kt % 4, a * TG:(a + 1) * TG],
                                   start=(m == 0), stop=(m == KT // 2 - 1), skip_group_check=True)
                mm.then_inc(S("PV"), 1)

            def o_t(it, u, last_head=False):
                wait(pe, "oe", it, HB, u + 1)
                if last_head:
                    wait(pe, "os", it, HB, u)
                else:
                    wait(pe, "mTc", it, HB, u + 3)
                for j in range(TT):
                    m = pe.transpose(b7[:, j * P:(j + 1) * P], o_sb[:, u % 2, j * P:(j + 1) * P], ident[:, :])
                m.then_inc(S("ot"), 1)

            def m_t(it, u):
                wait(pe, "nmp", it, HB, u + 1)
                wait(pe, "os", it, HB, u - 2)
                pe.transpose(m_tr, nmp[:, u, :, :].rearrange("p i t -> p (i t)"), ident_b[:, :])\
                    .then_inc(S("mT"), 1)

            def att(it, first, last):
                for u in range(HB):
                    prev = (it, u - 1) if u else (it - 1, HB - 1)
                    has_prev = not (first and u == 0)
                    wait(pe, f"m_ld{u}", it, 16, 16)
                    for kt in range(KT):
                        scores(it, u, 2 * kt)
                        scores(it, u, 2 * kt + 1)
                        m = u + 2
                        if m < HB:
                            max_scores(it, m, kt)
                        elif not last:
                            max_scores(it + 1, m - HB, kt)
                        if kt == 1 and has_prev:
                            pv(*prev, KT // 2 - 1)
                        if kt == 2:
                            if u + 1 < HB:
                                m_t(it, u + 1)
                            elif not last:
                                m_t(it + 1, 0)
                        if kt == 4 and has_prev:
                            o_t(*prev, last_head=(last and u == HB - 1))
                        if kt >= 3 and kt % 2 == 1:
                            pv(it, u, (kt - 3) // 2)

            pe.wait_ge(S("stt"), NG * E)
            pe.wait_ge(S("h32"), NG * HT)
            pe.wait_ge(S("kf"), NG)
            pe.wait_ge(S("vd"), NG)
            for u in range(2):
                for t in range(NT):
                    max_scores(0, u, t)
            m_t(0, 0)
            pe.wait_ge(S("mTc"), 1)
            att(0, True, False)
            with pe.Fori(1, NIT - 1) as it:
                att(it, False, False)
            att(NIT - 1, False, True)
            pv(NIT - 1, HB - 1, KT // 2 - 1)
            o_t(NIT - 1, HB - 1, last_head=True)

            def msa_turn(g):
                wait(pe, "tmc", 0, 0, g - 1)
                for t in range(TT):
                    m = pe.transpose(bank[g % 2][:, t * P:(t + 1) * P], msa[:, g * TT + t, :], ident[:, :])
                m.then_inc(S("tm"), 1)

            def project(g):
                wait(pe, "tmc", 0, 0, g + 1)
                wait(pe, "y", 0, 0, g - 1)
                pe.matmul(bank[2 + g % 2][:, :], wp_sb[:, :], msaT[:, g % 2, :], start=True, stop=True)\
                    .then_inc(S("tp"), 1)

            def y_turn(g):
                wait(pe, "yg", 0, 0, g + 1)
                wait(pe, "ty", 0, 0, g - 1)
                for t in range(TT):
                    m = pe.transpose(bank[4 + g % 2][:, t * P:(t + 1) * P], y2[:, g % 2, t * P:(t + 1) * P],
                                     ident[:, :])
                m.then_inc(S("tt"), 1)

            pe.wait_ge(S("msa"), NHEAD)
            for g in range(NG + 2):
                if g < NG:
                    msa_turn(g)
                if 1 <= g <= NG:
                    project(g - 1)
                if g >= 2:
                    y_turn(g - 2)

        @block.vector
        def _(dve):
            dve.memset(q_st[64:P, :, :], 0.0).then_inc(S("zeros"), 1)
            dve.memset(k_st[64:QROWS, :, :], 0.0).then_inc(S("zeros"), 1)
            dve.memset(k_st[QROWS:P, :, :], 1.0).then_inc(S("zeros"), 1)
            dve.memset(zero8[:, :], 0.0).then_inc(S("zeros"), 1)
            ch = Chain(dve, S("dve"))

            def rsqrt():
                v, y, hv, a = (nwt[:, i, :] for i in range(4))
                ch.mark(dve.tensor_scalar(v, mv[:, :, 1], EPS, None, ALU.add))
                ch.sync()
                ch.mark(dve.tensor_scalar(guess[:, :], v.bitcast(I32), 1, None, ALU.logical_shift_right))
                ch.mark(dve.tensor_scalar(hv, v, -0.5, None, ALU.mult))
                ch.sync()
                ch.mark(dve.tensor_scalar(y.bitcast(I32), guess[:, :], -1.0, float(RSQRT_GUESS), ALU.mult, ALU.add))
                for _ in range(NEWTON):
                    ch.sync()
                    ch.mark(dve.tensor_tensor(a, y, y, ALU.mult))
                    ch.sync()
                    ch.mark(dve.tensor_tensor(a, a, hv, ALU.mult))
                    ch.sync()
                    ch.mark(dve.scalar_tensor_tensor(y, a, 1.5, y, ALU.add, ALU.mult))

            def stats(src):
                for t in range(TT):
                    i = dve.bn_stats(st1[:, t, :], src[:, t, :])
                ch.mark(i)
                ch.sync()
                for t in range(TT):
                    i = dve.bn_aggr(mv[:, t, :], st1[:, t, :])
                ch.mark(i)
                ch.sync()

            def pre(g):
                def x_stats():
                    wait(dve, "x", g, 16, 16)
                    stats(xz)

                def normalise(done):
                    def step():
                        ch.sync()
                        if done == "zn":
                            wait(dve, "t1", g, 1, 1)
                        for t in range(TT):
                            i = dve.tensor_scalar(xz[:, t, :], xz[:, t, :], mv[:, t, 0:1], nwt[:, 1, t:t + 1],
                                                  ALU.subtract, ALU.mult)
                        i.then_inc(S(done), 1)
                    return step

                def z_stats():
                    wait(dve, "xn", g, 1, 1)
                    stats(xz)

                def high_x():
                    wait(dve, "xnT", g, 1, 1)
                    dve.tensor_copy(G(xh, g), xnT[:, :]).then_inc(S("xh"), 1)
                    wait(dve, "xh", g, 1, 1)
                    dve.tensor_tensor(G(xl, g), xnT[:, :], G(xh, g).bitcast(F32), ALU.subtract)\
                        .then_inc(S("xl"), 1)

                def router_top():
                    wait(dve, "lg", g, 1, 1)
                    ch.mark(dve.tensor_tensor(lg[:, :, :], b7[:, 0:TT * E].rearrange("p (t e) -> p t e", e=E),
                                              br_bc[:, :].unsqueeze(1).broadcast_to([P, TT, E]), ALU.add))
                    ch.sync()
                    for t in range(TT):
                        i = dve.max(top[:, t, :], lg[:, t, :])
                    ch.mark(i)
                    ch.sync()
                    dve.tensor_tensor(rt[:, 0, :, :], lg[:, :, :], top[:, :, 0:1].broadcast_to([P, TT, E]),
                                      ALU.subtract).then_inc(S("dlt"), 1)
                    ch.mark(dve.tensor_tensor(rt[:, 2, :, :], lg[:, :, :], top[:, :, 1:2].broadcast_to([P, TT, E]),
                                              ALU.is_ge))

                def router_weights():
                    wait(dve, "th", g, 1, 1)
                    ch.mark(dve.tensor_scalar(rt[:, 3, :, :], rt[:, 1, :, :], 1.0, None, ALU.add))
                    ch.mark(dve.tensor_scalar(rt[:, 4, :, :], rt[:, 1, :, :], -1.0, 1.0, ALU.mult, ALU.add))
                    ch.sync()
                    ch.mark(dve.reciprocal(rt[:, 4, :, :], rt[:, 4, :, :]))
                    ch.sync()
                    ch.mark(dve.tensor_tensor(rt[:, 3, :, :], rt[:, 3, :, :], rt[:, 4, :, :], ALU.mult))
                    ch.sync()
                    ch.mark(dve.tensor_tensor(rt[:, 3, :, :], rt[:, 3, :, :], rt[:, 2, :, :], ALU.mult))
                    ch.sync()
                    ch.mark(dve.tensor_reduce(rs[:, 0, :], rt[:, 3, :, :], AX.X, ALU.add))
                    ch.sync()
                    ch.mark(dve.reciprocal(rs[:, 1, :], rs[:, 0, :]))
                    ch.sync()
                    wait(dve, "wt", g, 1, 0)
                    dve.tensor_tensor(rt[:, 5, :, :], rt[:, 3, :, :],
                                      rs[:, 1, :].unsqueeze(2).broadcast_to([P, TT, E]), ALU.mult)\
                        .then_inc(S("w"), 1)
                    ch.end()

                def second(w):
                    def step():
                        wait(dve, "r1", g, 2, w + 1)
                        dve.tensor_copy(qkp[:, w, 1, :], qkf[:, w, :]).then_inc(S("p1"), 1)
                    return step

                def values():
                    wait(dve, "v", g, 1, 1)
                    dst = v_sb[:, g * TT:(g + 1) * TT, :] if isinstance(g, int) else v_sb[:, bass.ds(g * TT, TT), :]
                    dve.tensor_tensor(dst, b7[:, :].rearrange("p (t d) -> p t d", d=D),
                                      bv_bc[:, :].unsqueeze(1).broadcast_to([P, TT, D]), ALU.add)\
                        .then_inc(S("vd"), 1)
                return {1: [x_stats], 3: [rsqrt], 5: [normalise("xn")], 7: [z_stats], 9: [rsqrt],
                        11: [normalise("zn")], 13: [high_x], 17: [router_top], 20: [router_weights],
                        24: [second(0)], 25: [second(1)], HT + 1: [values]}

            def experts(g):
                def low_h(i):
                    def step():
                        wait(dve, "h32", g, HT, i + 1)
                        wait(dve, "m2", g, HT, max(i - 3, 0))
                        dve.tensor_tensor(hl[:, i % 4, :], h32[:, i % 2, :], hh[:, i % 4, :].bitcast(F32),
                                          ALU.subtract).then_inc(S("hl"), 1)
                    return step

                def combine(e):
                    def step():
                        wait(dve, "m2", g, HT, (e + 1) * HC)
                        if isinstance(g, int):
                            dve.wait_ge(s_wbc[e], 16 * (g + 1))
                        else:
                            dve.wait_ge(s_wbc[e], 16 * g + 16)
                        if e:
                            wait(dve, "acc", g, E - 1, max(e - 2, 0))
                        dst = prod[:, e % 2, :] if e else acc[:, :]
                        dve.scalar_tensor_tensor(dst, bank[2 + e % 2][:, :], col(C_B2 + e), wbc[:, e, :],
                                                 ALU.add, ALU.mult).then_inc(S("stt"), 1)
                    return step
                def total():
                    wait(dve, "stt", g, E, E)
                    wait(dve, "acc", g, E - 1, E - 2)
                    dve.tensor_tensor(G(ffn, g), acc[:, :], prod[:, (E - 1) % 2, :], ALU.add).then_inc(S("acc"), 1)

                plan = {4 * e + 6: [combine(e)] for e in range(E)}
                plan[4 * E + 4] = [total]
                for i in range(HT):
                    plan.setdefault(i, []).append(low_h(i))
                return plan

            run_slots(NSLOT, pre(0))
            run_slots(NSLOT, experts(0), pre(1))
            with dve.Fori(1, NG - 1) as g:
                run_slots(NSLOT, experts(g), pre(g + 1))
            run_slots(NSLOT, experts(NG - 1))

            def row_max(it, u, t):
                wait(dve, "M", it, HB * NT, u * NT + t + 1)
                pair = wide_banks[t % 2]
                dve.tensor_reduce(mx[:, u, t:t + 1], pair, AX.X, ALU.max, negate=True).then_inc(S("R"), 1)

            def head_out(it, u):
                wait(dve, "ot", it, HB, u + 1)
                turned = b7[:, :].rearrange("p (j k a r) -> p a j r k", k=2, a=2, r=VC)
                for a in range(2):
                    i = dve.tensor_reduce(o9[:, u % 2, a * TT:(a + 1) * TT, :], turned[:, a, :, 0:DH + 1, :],
                                          AX.X, ALU.add)
                i.then_inc(S("os"), 1)
                wait(dve, "os", it, HB, u + 1)
                dve.reciprocal(rden[:, u % 2, :], o9[:, u % 2, :, DH]).then_inc(S("rd"), 1)
                wait(dve, "rd", it, HB, u + 1)
                b, h = it // (H // HB), (it % (H // HB)) * HB + u
                dst = msa[:, b * NT:(b + 1) * NT, h * DH:(h + 1) * DH] if isinstance(it, int) else \
                    msa[:, bass.ds(b * NT, NT), bass.ds(h * DH, DH)]
                dve.tensor_tensor(dst, o9[:, u % 2, :, 0:DH], rden[:, u % 2, :].unsqueeze(2)
                                  .broadcast_to([P, NT, DH]), ALU.mult).then_inc(S("msa"), 1)

            def att(it, first, last):
                for u in range(HB):
                    for t in range(NT):
                        m = u + 2
                        if m < HB:
                            row_max(it, m, t)
                        elif not last:
                            row_max(it + 1, m - HB, t)
                        if t == 4 and not (first and u == 0):
                            head_out(*((it, u - 1) if u else (it - 1, HB - 1)))

            for u in range(2):
                for t in range(NT):
                    row_max(0, u, t)
            att(0, True, False)
            with dve.Fori(1, NIT - 1) as it:
                att(it, False, False)
            att(NIT - 1, False, True)
            head_out(NIT - 1, HB - 1)

            dve.wait_ge(S("gate"), 1)

            def gated(g):
                k = g % 2
                wait(dve, "tp", 0, 0, g + 1)
                dve.scalar_tensor_tensor(y1[:, k, :], bank[2 + k][:, :], col(C_BP), xh[:, g, :].bitcast(F32),
                                         ALU.add, ALU.add).then_inc(S("y"), 1)
                wait(dve, "y", 0, 0, g + 1)
                wait(dve, "tt", 0, 0, g - 1)
                dve.tensor_tensor(y2[:, k, :], y1[:, k, :], xl[:, g, :].bitcast(F32), ALU.add).then_inc(S("ya"), 1)
                wait(dve, "ya", 0, 0, g + 1)
                dve.tensor_tensor(y2[:, k, :], y2[:, k, :], ffn[:, g, :], ALU.mult).then_inc(S("yg"), 1)

            def finish(g):
                k = g % 2
                wait(dve, "tt", 0, 0, g + 1)
                wait(dve, f"tx{k}", 0, 0, 16 * (g // 2 + 1))
                dst = x_out[:, k, :, :]
                dve.tensor_tensor(dst, bank[4 + k][:, :].rearrange("p (t d) -> p t d", d=D), dst, ALU.add)\
                    .then_inc(S("ty"), 1)
            for g in range(NG + 1):
                if g < NG:
                    gated(g)
                if g:
                    finish(g - 1)


_INS = ["L0_attn_z", "L0_attn_ln_w", "L0_attn_ln_b", "L0_attn_W_qkv", "L0_attn_b_qkv", "L0_attn_W_proj",
        "L0_attn_b_proj", "L0_ffn_W1", "L0_ffn_b1", "L0_ffn_W2", "L0_ffn_b2", "L0_ffn_Wr", "L0_ffn_br"]


def kernel(**inputs):
    import numpy as _np
    import concourse.bacc as _bacc
    from concourse import mybir as _mybir
    from concourse.bass_utils import run_bass_kernel_spmd as _run

    nc = _bacc.Bacc("TRN2", target_bir_lowering=False, num_devices=1)
    arrays, args = {}, []
    for name in _INS:
        a = _np.ascontiguousarray(inputs[name])
        arrays[f"in_{name}_dram"] = a
        args.append(nc.dram_tensor(f"in_{name}_dram", a.shape, _mybir.dt.from_np(a.dtype), kind="ExternalInput").ap())
    shape = inputs["L0_attn_z"].shape
    args.append(nc.dram_tensor("out_0_dram", shape, _mybir.dt.float32, kind="ExternalOutput").ap())
    attention_and_experts(nc, *args)
    r = _run(nc, [arrays], core_ids=[0])
    return r.results[0]["out_0_dram"]
```

```python
from contextlib import ExitStack

import concourse.bass as bass
from concourse import mybir

ALU = mybir.AluOpType
ACT = mybir.ActivationFunctionType
AX = mybir.AxisListType
F32 = mybir.dt.float32
F32R = mybir.dt.float32r
BF16 = mybir.dt.bfloat16
I32 = mybir.dt.int32

P = 128
TG = 512
TT = TG // P
PARTS = 3
QROWS = 96
SROWS = QROWS + PARTS
VC = 32
EPS = 1e-5
RSQRT_GUESS = 0x5F3759DF
NEWTON = 3


class Chain:

    def __init__(self, eng, sem):
        self.eng, self.sem, self.n = eng, sem, 0

    def mark(self, ins):
        self.n += 1
        ins.then_inc(self.sem, 1)

    def sync(self):
        self.eng.wait_ge(self.sem, self.n)

    def end(self):
        self.sync()
        self.eng.sem_inc(self.sem, -self.n)
        self.n = 0


def run_slots(slots, *plans):
    for s in slots:
        for plan, shift in plans:
            for step in plan.get(s + shift, []):
                step()


def attention_and_experts(nc, x, ln_w, ln_b, w_qkv, b_qkv, w_proj, b_proj, w1, b1, w2, b2, w_r, b_r, out):
    B, N, D = x.shape
    E, _, HID = w1.shape
    H = 16
    DH = D // H
    SCALE = float(DH) ** -0.5
    NG = B * N // TG
    HC = HID // P
    HT = E * HC
    KT = N // P
    NT = N // P
    NHEAD = B * H
    HB = 4
    RAW = 8
    NIT = NHEAD // HB
    LAG = 6
    assert D == P and N % TG == 0 and N // TG == 2 and HID % P == 0

    x_g = x.rearrange("b (g t p) d -> (b g) p t d", p=P, t=TT)
    out_g = out.rearrange("b (g t p) d -> (b g) p t d", p=P, t=TT)

    q_dram = nc.dram_tensor("q_parts_dram", (B, D, PARTS, N), BF16, kind="Internal").ap()
    k_dram = nc.dram_tensor("k_parts_dram", (PARTS, B, D, PARTS, N), BF16, kind="Internal").ap()
    w_dram = nc.dram_tensor("expert_w_dram", (NG, TT, E, P), F32, kind="Internal").ap()
    m_dram = nc.dram_tensor("neg_max_dram", (HB, PARTS * NT, P), BF16, kind="Internal").ap()
    q_rows = q_dram.rearrange("b r i t -> (b r i) t")
    k_rows = k_dram.rearrange("j b r i t -> j (b r i) t")

    with ExitStack() as ctx:
        def sb(name, shape, dt=F32, c=ctx):
            return c.enter_context(nc.sbuf_tensor(name, shape, dt))

        def sem(name):
            return ctx.enter_context(nc.semaphore(name))

        xh = sb("xn_t_hi", [P, NG, TG], F32R)
        xl = sb("xn_t_lo", [P, NG, TG], F32R)
        ffn = sb("ffn_t", [P, NG, TG])
        v_sb = sb("v_sb", [P, B * KT, D])
        q_st = sb("q_stack", [P, HB, N], BF16)
        k_st = sb("k_stack", [P, HB, N], BF16)
        ident = sb("ident", [P, P])
        ident_b = sb("ident_b", [P, P], BF16)
        cols = sb("cols", [P, 64])
        zero8 = sb("zero8", [P, NT])

        mx = sb("neg_max", [P, HB, NT])
        nm = sb("neg_max_rest", [P, HB, NT])
        nmp = sb("neg_max_parts", [P, HB, PARTS, NT], BF16)

        ffn_ctx = ExitStack()
        fs = lambda name, shape, dt=F32: sb(name, shape, dt, ffn_ctx)
        w1h = fs("w1_hi", [P, E, HID], F32R)
        w1l = fs("w1_lo", [P, E, HID], F32R)
        w2h = fs("w2_hi", [P, E, HC * D], F32R)
        w2l = fs("w2_lo", [P, E, HC * D], F32R)
        wbc = fs("expert_w_bc", [P, E, TG])
        hh = fs("h_hi", [P, 4, TG], F32R)
        hl = fs("h_lo", [P, 4, TG], F32R)
        h32 = fs("h_full", [P, 2, TG])
        prod = fs("prod", [P, 2, TG])
        acc = fs("acc", [P, TG])
        xz = fs("xz", [P, TT, D])
        xnT = fs("xn_t", [P, TG])
        znT = fs("zn_t", [P, TG])
        qkf = fs("qk_full", [P, 2, TG])
        qkp = fs("qk_parts", [P, 2, PARTS, TG], BF16)
        wqkv_sb = fs("wqkv_sb", [P, 3 * D])
        wr_sb = fs("wr_sb", [P, E])
        bv_bc = fs("bv_bc", [P, D])
        br_bc = fs("br_bc", [P, E])
        st1 = fs("bn_parts", [P, TT, 6])
        mv = fs("mean_var", [P, TT, 2])
        nwt = fs("newton", [P, 4, TT])
        guess = fs("guess", [P, TT], I32)
        lg = fs("logits", [P, TT, E])
        top = fs("top8", [P, TT, 8])
        rt = fs("router", [P, 6, TT, E])
        rs = fs("router_sum", [P, 2, TT])
        wT = fs("w_t", [TT * E, P])
        rows = acc[0:48, 0:P]
        nmT = wT[0:PARTS * NT, :].bitcast(BF16).rearrange("k (s p) -> k s p", s=2)
        ffn_ctx.close()
        w_raw = ffn

        att_ctx = ExitStack()
        ats = lambda name, shape, dt=F32: sb(name, shape, dt, att_ctx)
        p_sb = ats("p_ring", [P, 4, N])
        v_st = ats("v_stack", [P, HB, KT, VC])
        wp_sb = ats("wp_sb", [P, D])
        o_sb = ats("o_sb", [P, 2, TG])
        o9 = ats("o_sum", [P, 2, NT, DH + 1])
        rden = ats("rden", [P, 2, NT])
        msa = ats("msa", [P, B * NT, D])
        msaT = ats("msa_t", [P, 2, TG])
        y1 = ats("y1", [P, 2, TG])
        y2 = ats("y2", [P, 2, TG])
        x_out = ats("x_out", [P, 2, TT, D])
        att_ctx.close()

        psum = ctx.enter_context(nc.psum_tensor("psum", [P, 8 * TG], F32))
        bank = [psum[:, i * TG:(i + 1) * TG] for i in range(8)]
        wide_banks = [psum[:, (2 + 2 * i) * TG:(4 + 2 * i) * TG] for i in range(2)]
        b5, b6, b7 = bank[5], bank[6], bank[7]
        ring = [bank[0], bank[1], bank[7]]
        RING = [("P", i) for i in range(2 * KT)]
        RING.insert(RING.index(("P", 5)), ("mTc", 0))
        RING.insert(RING.index(("P", 9)), ("os", 0))
        assert len(RING) % len(ring) == 0

        def ring_bank(name, i=0):
            return ring[RING.index((name, i)) % len(ring)]

        C_B1, C_B2 = 0, HT
        C_LNW, C_LNB, C_BQ, C_BK, C_BP = (HT + E + i for i in range(5))
        NROW = HT + E + 5

        def col(i):
            return cols[:, i:i + 1]

        s = {}

        def S(name):
            if name not in s:
                s[name] = sem("s_" + name)
            return s[name]

        for name in ("const w_raw0 w_raw1 w_raw2 w_raw3 w_raw4 w_raw5 w_raw6 w_raw7 w_hi w_lo_v w_lo_p guess nwt rows ident zeros cols_t cols x xn zn t1 t2 "
                     "xnT znT xh xl lg dlt th w wt wT w_st qp_st q k v qf kf p0 r1 p1 qp vd "
                     "h hh h32 hl m2 stt acc gate dve pool "
                     "S P PV M R nmp mT mTc m_st m_ld0 m_ld1 m_ld2 m_ld3 st0 st1 st2 st3 vst oe ot os msa "
                     "wp adve apool tm tmc tp y ya yg tt ty rd tx0 tx1 out0 out1 vinit tdve").split():
            S(name)
        s_wbc = [sem(f"s_wbc{e}") for e in range(E)]

        def wait(eng, name, it, per, k):
            if isinstance(it, int):
                if it * per + k > 0:
                    eng.wait_ge(S(name), it * per + k)
            else:
                eng.wait_ge(S(name), it * per + k)

        def weights_lo(eng, n):
            e, slot = n // 2, n % RAW
            hi, lo = ((w1h, w1l), (w2h, w2l))[n % 2]
            eng.wait_ge(S("w_hi"), n + 1)
            eng.tensor_tensor(lo[:, e, :], w_raw[:, slot, :], hi[:, e, :].bitcast(F32), ALU.subtract)\
                .then_inc(S("w_lo_v" if n < RAW else "w_lo_p"), 1)

        def G(t, g):
            return t[:, g, :] if isinstance(g, int) else t[:, bass.ds(g, 1), :].rearrange("p a t -> p (a t)")

        block = ctx.enter_context(nc.Block())

        def expert_phase(eng, experts, pre, first=None, extra=None):
            full = range(HT)

            def body(g, carry=True):
                plans = [(pre(g + 1), 0), (experts(g), 0)]
                if isinstance(g, int) and g == 0:
                    plans.insert(0, (first or {}, 0))
                if carry:
                    plans.insert(0, (experts(g - 1), HT))
                run_slots(full, *plans)
            body(0, carry=False)
            with eng.Fori(1, NG - 1) as g:
                body(g)
            last = NG - 1
            run_slots(full, (experts(last - 1), HT), (extra or {}, 0), (experts(last), 0))
            run_slots(range(LAG), (extra or {}, HT), (experts(last), HT))

        QP_ST = 6 * 16

        def sp_weight(sp, n):
            e, slot = n // 2, n % RAW
            if n >= RAW:
                sp.wait_ge(S("w_lo_v"), n - RAW + 1)
            dst = w_raw[:, slot, :]
            if n % 2 == 0:
                sp.dma_start(dst, w1[e, :, :]).then_inc(S(f"w_raw{slot}"), 16)
            else:
                sp.dma_start(dst.rearrange("p (c d) -> p c d", c=HC),
                             w2[e, :, :].rearrange("(c p) d -> p c d", p=P)).then_inc(S(f"w_raw{slot}"), 16)

        def sp_load_x(sp, g):
            def step():
                wait(sp, "t2", g, 1, 0)
                src = x_g[g] if isinstance(g, int) else x_g[bass.ds(g, 1)].rearrange("a p t d -> (a p) t d")
                sp.dma_start(xz[:, :, :], src).then_inc(S("x"), 16)
            return step

        def sp_pre(sp, g):
            b, half = (g // 2, g % 2)

            def store_w():
                wait(sp, "wT", g, 1, 1)
                dst = w_dram[g] if isinstance(g, int) else w_dram[bass.ds(g, 1)].rearrange("a t e p -> (a t) e p")
                sp.dma_start(dst.rearrange("t e p -> (t e) p"), wT[:, :]).then_inc(S("w_st"), 16)

            def cut(t, bb):
                return t[bb] if isinstance(bb, int) else t[bass.ds(bb, 1)].rearrange("a r i t -> (a r) i t")

            def store_q():
                wait(sp, "qp", g, 2, 1)
                sp.dma_start(cut(q_dram, b)[:, :, tok(half)], qkp[:, 0, :, :]).then_inc(S("qp_st"), 16)

            def store_k():
                wait(sp, "qp", g, 2, 2)
                for j in range(PARTS):
                    dst = cut(k_dram[j], b)[:, :, tok(half)]
                    sp.dma_start(dst[:, 0:PARTS - j, :], qkp[:, 1, j:PARTS, :]).then_inc(S("qp_st"), 16)
                    if j:
                        sp.dma_start(dst[:, PARTS - j:PARTS, :], qkp[:, 1, 0:j, :]).then_inc(S("qp_st"), 16)

            def tok(hf):
                return slice(hf * TG, (hf + 1) * TG) if isinstance(hf, int) else bass.ds(hf * TG, TG)

            return [store_w], [store_q, store_k]

        def sp_wbc(sp, g, e):
            def step():
                if e == 0:
                    wait(sp, "w_st", g, 16, 16)
                wait(sp, "stt", g, E, e + 1 - E)
                src = w_dram[g, :, e, :] if isinstance(g, int) else \
                    w_dram[bass.ds(g, 1), :, e, :].rearrange("a t p -> (a t) p")
                sp.dma_start(wbc[:, e, :].rearrange("p (t c) -> p t c", t=TT), src.partition_broadcast(P))\
                    .then_inc(s_wbc[e], 16)
            return step

        def sp_stage(sp, n, u):
            r0 = n * (DH * PARTS)

            def rows_of(t):
                return t[r0:r0 + DH * PARTS, :] if isinstance(n, int) else t[bass.ds(r0, DH * PARTS), :]
            for j in range(PARTS):
                lo = j * DH * PARTS
                sp.dma_start(q_st[lo:lo + DH * PARTS, u, :], rows_of(q_rows)).then_inc(S(f"st{u}"), 16)
                sp.dma_start(k_st[lo:lo + DH * PARTS, u, :], rows_of(k_rows[j])).then_inc(S(f"st{u}"), 16)

        def sp_att(sp, it, last):
            for u in range(HB):
                m = u + 1
                if not (last and m >= HB):
                    slot, mit = m % HB, it + m // HB
                    wait(sp, "mTc", mit, HB, slot + 1)
                    sp.dma_start(m_dram[slot], nmT[:, slot % 2, :]).then_inc(S("m_st"), 16)
                    wait(sp, "m_st", mit, HB * 16, (slot + 1) * 16)
                    sp.dma_start(q_st[QROWS:SROWS, slot, :],
                                 m_dram[slot].rearrange("(i t) c -> i (t c)", i=PARTS)).then_inc(S(f"m_ld{slot}"), 16)
                if not last:
                    wait(sp, "S", it, HB * 2 * KT, (u + 1) * 2 * KT)
                    sp_stage(sp, (it + 1) * HB + u, u)

        @block.sync
        def _(sp):
            sp_load_x(sp, 0)()
            for r0, r1, src in ((0, HT, b1.rearrange("e (c p) -> (e c) p", p=P)), (HT, HT + E, b2),
                                (C_LNW, C_LNW + 1, ln_w.rearrange("(a p) -> a p", a=1)),
                                (C_LNB, C_LNB + 1, ln_b.rearrange("(a p) -> a p", a=1)),
                                (C_BQ, C_BQ + 2, b_qkv[0:2 * D].rearrange("(a p) -> a p", p=P)),
                                (C_BP, C_BP + 1, b_proj.rearrange("(a p) -> a p", a=1))):
                sp.dma_start(rows[r0:r1, :], src).then_inc(S("rows"), 16)
            sp.dma_start(wqkv_sb[:, :], w_qkv).then_inc(S("const"), 16)
            sp.dma_start(wr_sb[:, :], w_r).then_inc(S("const"), 16)
            sp.dma_start(bv_bc[:, :], b_qkv[2 * D:3 * D].partition_broadcast(P)).then_inc(S("const"), 16)
            sp.dma_start(br_bc[:, :], b_r.partition_broadcast(P)).then_inc(S("const"), 16)
            for n in range(RAW):
                sp_weight(sp, n)
            sp_load_x(sp, 1)()

            def spread_w(g):
                for f in sp_pre(sp, g)[0]:
                    f()
                for e in range(E):
                    sp_wbc(sp, g, e)()

            def store_qk(g):
                for f in sp_pre(sp, g)[1]:
                    f()

            spread_w(0)
            for n in range(RAW, 2 * E):
                sp_weight(sp, n)
            store_qk(0)

            def body(g):
                store_w = sp_pre(sp, g)[0]
                for f in store_w:
                    f()
                store_qk(g)
                if not (isinstance(g, int) and g == NG - 1):
                    sp_load_x(sp, g + 1)()
                for e in range(E):
                    sp_wbc(sp, g, e)()

            with sp.Fori(1, NG - 1) as g:
                body(g)
            sp.wait_ge(S("zeros"), 4)
            sp.wait_ge(S("qp_st"), (NG - 1) * QP_ST)
            for u in range(HB):
                sp_stage(sp, u, u)
            body(NG - 1)
            sp.wait_ge(S("qp_st"), NG * QP_ST)
            sp.wait_ge(S("mTc"), 1)
            sp.dma_start(m_dram[0], nmT[:, 0, :]).then_inc(S("m_st"), 16)
            sp.wait_ge(S("m_st"), 16)
            sp.dma_start(q_st[QROWS:SROWS, 0, :], m_dram[0].rearrange("(i t) c -> i (t c)", i=PARTS))\
                .then_inc(S("m_ld0"), 16)
            sp.wait_ge(S("m2"), NG * HT)
            sp.dma_start(wp_sb[:, :], w_proj).then_inc(S("wp"), 16)
            sp_att(sp, 0, False)
            with sp.Fori(1, NIT - 1) as it:
                sp_att(sp, it, False)
            sp_att(sp, NIT - 1, True)

            for g in range(NG):
                k = g % 2
                if g >= 2:
                    wait(sp, "ty", 0, 0, g - 1)
                    sp.dma_start(out_g[g - 2], x_out[:, k, :, :]).then_inc(S(f"out{k}"), 16)
                    wait(sp, f"out{k}", 0, 0, 16 * (g // 2))
                sp.dma_start(x_out[:, k, :, :], x_g[g]).then_inc(S(f"tx{k}"), 16)
            for g in (NG - 2, NG - 1):
                wait(sp, "ty", 0, 0, g + 1)
                sp.dma_start(out_g[g], x_out[:, g % 2, :, :]).then_inc(S(f"out{g % 2}"), 16)
            for k in (0, 1):
                sp.wait_ge(S(f"out{k}"), 16 * (NG // 2))
            sp.wait_ge(S("qp_st"), NG * QP_ST)
            sp.wait_ge(S("w_st"), NG * 16)
            sp.wait_ge(S("m_st"), NHEAD * 16)

        @block.gpsimd
        def _(pool):
            for n, t in enumerate((ident, ident_b)):
                pool.memset(t[:, :], 0.0).then_inc(S("pool"), 1)
                pool.wait_ge(S("pool"), n + 1)
                pool.affine_select(out=t[:, :], in_=t[:, :], compare_op=ALU.not_equal, fill=1.0, base=0,
                                   pattern=[[-1, P]], channel_multiplier=1).then_inc(S("ident"), 1)
            ch = Chain(pool, S("apool"))

            def pre(g):
                def rest(w):
                    def step():
                        wait(pool, "p0", g, 2, w + 1)
                        pool.tensor_tensor(qkf[:, w, :], qkf[:, w, :], qkp[:, w, 0, :], ALU.subtract)\
                            .then_inc(S("r1"), 1)
                    return step

                def third(w):
                    def step():
                        wait(pool, "p1", g, 2, w + 1)
                        pool.tensor_tensor(qkp[:, w, 2, :], qkf[:, w, :], qkp[:, w, 1, :], ALU.subtract)\
                            .then_inc(S("qp"), 1)
                    return step
                return {4: [newton(g, 1)], 12: [newton(g, 2)], 23: [rest(0)], 24: [rest(1)],
                        27: [third(0)], 28: [third(1)]}

            def neg_parts(it, u):
                wait(pool, "R", it, HB * NT, (u + 1) * NT)
                a, r = mx[:, u, :], nm[:, u, :]
                p = [nmp[:, u, i, :] for i in range(PARTS)]
                ch.mark(pool.tensor_tensor(p[0], a, zero8[:, :], ALU.add))
                ch.sync()
                ch.mark(pool.tensor_tensor(r, a, p[0], ALU.subtract))
                ch.sync()
                ch.mark(pool.tensor_copy(p[1], r))
                ch.end()
                pool.tensor_tensor(p[2], r, p[1], ALU.subtract).then_inc(S("nmp"), 1)

            def newton(g, k):
                def step():
                    y, hv, a = (nwt[:, i, :] for i in (1, 2, 3))
                    wait(pool, "guess", g, 2, k)
                    for n in range(NEWTON):
                        ch.mark(pool.tensor_tensor(a, y, y, ALU.mult))
                        ch.sync()
                        ch.mark(pool.tensor_tensor(a, a, hv, ALU.mult))
                        ch.sync()
                        ch.mark(pool.tensor_scalar(a, a, 1.5, None, ALU.add))
                        if n < NEWTON - 1:
                            ch.sync()
                            ch.mark(pool.tensor_tensor(y, y, a, ALU.mult))
                            ch.sync()
                    ch.end()
                    pool.tensor_tensor(y, y, a, ALU.mult).then_inc(S("nwt"), 1)
                return step

            def experts(g):
                def add(e):
                    def step():
                        wait(pool, "stt", g, E, e + 1)
                        if e > 1:
                            wait(pool, "acc", g, E - 1, e - 1)
                        pool.tensor_tensor(acc[:, :], acc[:, :], prod[:, e % 2, :], ALU.add).then_inc(S("acc"), 1)
                    return step
                return {4 * e + 7: [add(e)] for e in range(1, E - 1)}

            run_slots(range(HT), (pre(0), 0))
            expert_phase(pool, experts, pre,
                         first={n - 3: [lambda n=n: weights_lo(pool, n)] for n in range(RAW, 2 * E)},
                         extra={17: [lambda: neg_parts(0, 0)], HT + 1: [lambda: neg_parts(0, 1)]})

            pool.wait_ge(S("m2"), NG * HT)
            pool.memset(v_st[:, :, :, DH + 1:VC], 0.0).then_inc(S("vinit"), 1)
            pool.memset(v_st[:, :, :, DH:DH + 1], 1.0).then_inc(S("vinit"), 1)
            def stage_v(it, u):
                b, h = it // (H // HB), (it % (H // HB)) * HB + u
                wait(pool, "PV", it, HB * KT // 2, (u + 1 - HB) * KT // 2)
                if isinstance(b, int):
                    src = v_sb[:, b * KT:(b + 1) * KT, h * DH:(h + 1) * DH]
                else:
                    src = v_sb[:, bass.ds(b * KT, KT), bass.ds(h * DH, DH)]
                pool.tensor_copy(v_st[:, u, :, 0:DH], src).then_inc(S("vst"), 1)

            def att(it, first, last):
                for u in range(HB):
                    if not (first and u == 0):
                        stage_v(it, u)
                    m = u + 2
                    if m < HB:
                        neg_parts(it, m)
                    elif not last:
                        neg_parts(it + 1, m - HB)

            pool.wait_ge(S("vd"), NG)
            stage_v(0, 0)
            att(0, True, False)
            with pool.Fori(1, NIT - 1) as it:
                att(it, False, False)
            att(NIT - 1, False, True)

        @block.scalar
        def _(act):
            act.wait_ge(S("cols_t"), 1)
            act.activation(cols[:, 0:NROW], b7[:, 0:NROW], ACT.Copy).then_inc(S("cols"), 1)

            def weights_hi(n):
                e, slot = n // 2, n % RAW
                hi = (w1h, w2h)[n % 2]
                act.wait_ge(S(f"w_raw{slot}"), 16 * (n // RAW + 1))
                act.activation(hi[:, e, :], w_raw[:, slot, :], ACT.Copy).then_inc(S("w_hi"), 1)

            def pre(g):
                def x_t():
                    wait(act, "t1", g, 1, 1)
                    wait(act, "xl", g, 1, 0)
                    wait(act, "lg", g, 1, 0)
                    act.activation(xnT[:, :], b5[:, :], ACT.Copy).then_inc(S("xnT"), 1)

                def z_t():
                    if isinstance(g, int) and g == 0:
                        act.wait_ge(S("cols"), 1)
                    wait(act, "t2", g, 1, 1)
                    wait(act, "v", g, 1, 0)
                    act.activation(znT[:, :], b6[:, :], ACT.Identity, scale=col(C_LNW), bias=col(C_LNB))\
                        .then_inc(S("znT"), 1)

                def qk(w):
                    def step():
                        wait(act, ("q", "k")[w], g, 1, 1)
                        wait(act, "qp", g, 2, w - 1)
                        bk, bias = ((b5, C_BQ), (b6, C_BK))[w]
                        act.activation(qkf[:, w, :], bk[:, :], ACT.Identity, bias=col(bias))\
                            .then_inc(S(("qf", "kf")[w]), 1)
                    return step

                def tanh():
                    wait(act, "dlt", g, 1, 1)
                    act.activation(rt[:, 1, :, :], rt[:, 0, :, :], ACT.Tanh, scale=0.5).then_inc(S("th"), 1)

                def w_t():
                    wait(act, "wt", g, 1, 1)
                    wait(act, "w_st", g, 16, 0)
                    act.activation(wT[:, :], b7[0:TT * E, 0:P], ACT.Copy).then_inc(S("wT"), 1)
                return {9: [x_t], 15: [tanh], 18: [z_t], 21: [qk(0)], 22: [qk(1)], 24: [w_t]}

            def experts(g):
                def gelu(i):
                    def step():
                        wait(act, "h", g, HT, i + 1)
                        wait(act, "m2", g, HT, i - 3)
                        e, c = i // HC, i % HC
                        act.activation(hh[:, i % 4, :], bank[i % 2][:, :], ACT.Gelu, bias=col(C_B1 + i))\
                            .then_inc(S("hh"), 1)
                        wait(act, "hl", g, HT, i - 1)
                        act.activation(h32[:, i % 2, :], bank[i % 2][:, :], ACT.Gelu, bias=col(C_B1 + i))\
                            .then_inc(S("h32"), 1)
                    return step
                return {i: [gelu(i)] for i in range(HT)}

            def neg_max_t(it, u, early=False):
                m_tr = (b7 if early else ring_bank("mTc"))[0:PARTS * NT, 0:P // 2].bitcast(BF16)
                wait(act, "mT", it, HB, u + 1)
                wait(act, "m_st", it, HB * 16, (u - 1) * 16)
                act.activation(nmT[:, u % 2, :], m_tr, ACT.Copy).then_inc(S("mTc"), 1)

            def hi(ns):
                return [lambda n=n: weights_hi(n) for n in ns]

            run_slots(range(HT), (pre(0), 0), ({9: hi(range(2)), 12: hi(range(2, RAW))}, 0))
            expert_phase(act, experts, pre, first={n - RAW: hi([n]) for n in range(RAW, 2 * E)},
                         extra={20: [lambda: (wait(act, "w_st", NG, 16, 0), neg_max_t(0, 0, early=True))]})

            def o_copy(it, u):
                wait(act, "PV", it, HB * KT // 2, (u + 1) * KT // 2)
                wait(act, "ot", it, HB, u - 1)
                act.activation(o_sb[:, u % 2, :], b6[:, :], ACT.Copy).then_inc(S("oe"), 1)

            def att(it, first, last):
                for u in range(HB):
                    for i in range(2 * KT):
                        kt, a = i // 2, i % 2
                        wait(act, "S", it, HB * 2 * KT, u * 2 * KT + i + 1)
                        if i % 4 == 0:
                            wait(act, "PV", it, HB * KT // 2, u * KT // 2 + kt // 2 - 1)
                        act.activation(p_sb[:, kt % 4, a * TG:(a + 1) * TG], ring_bank("P", i)[:, :], ACT.Exp,
                                       scale=SCALE).then_inc(S("P"), 1)
                        if i == 3:
                            if u:
                                o_copy(it, u - 1)
                            elif not first:
                                o_copy(it - 1, HB - 1)
                        if i == 4:
                            if u + 1 < HB:
                                neg_max_t(it, u + 1)
                            elif not last:
                                neg_max_t(it + 1, 0)

            att(0, True, False)
            with act.Fori(1, NIT - 1) as it:
                att(it, False, False)
            att(NIT - 1, False, True)
            o_copy(NIT - 1, HB - 1)

            for g in range(NG):
                k = g % 2
                act.activation(ffn[:, g, :], ffn[:, g, :], ACT.Silu).then_inc(S("gate"), 1)
                wait(act, "tm", 0, 0, g + 1)
                wait(act, "tp", 0, 0, g - 1)
                act.activation(msaT[:, k, :], bank[k][:, :], ACT.Copy).then_inc(S("tmc"), 1)

        @block.tensor
        def _(pe):
            pe.wait_ge(S("ident"), 2)
            pe.wait_ge(S("rows"), 6 * 16)
            pe.transpose(b7[:, 0:NROW], rows[0:NROW, :], ident[0:NROW, 0:NROW]).then_inc(S("cols_t"), 1)
            pe.wait_ge(S("const"), 4 * 16)

            def pre(g):
                def t1():
                    wait(pe, "xn", g, 1, 1)
                    wait(pe, "qf", g, 1, 0)
                    for t in range(TT):
                        m = pe.transpose(b5[:, t * P:(t + 1) * P], xz[:, t, :], ident[:, :])
                    m.then_inc(S("t1"), 1)

                def t2():
                    wait(pe, "zn", g, 1, 1)
                    wait(pe, "kf", g, 1, 0)
                    for t in range(TT):
                        m = pe.transpose(b6[:, t * P:(t + 1) * P], xz[:, t, :], ident[:, :])
                    m.then_inc(S("t2"), 1)

                def logits():
                    wait(pe, "xnT", g, 1, 1)
                    if isinstance(g, int) and g == 0:
                        pe.wait_ge(S("cols"), 1)
                    wait(pe, "vd", g, 1, 0)
                    for t in range(TT):
                        m = pe.matmul(b7[:, t * E:(t + 1) * E], xnT[:, t * P:(t + 1) * P], wr_sb[:, :],
                                      start=True, stop=True)
                    m.then_inc(S("lg"), 1)

                def qk():
                    wait(pe, "znT", g, 1, 1)
                    pe.matmul(b5[:, :], wqkv_sb[:, 0:D], znT[:, :], start=True, stop=True).then_inc(S("q"), 1)
                    pe.matmul(b6[:, :], wqkv_sb[:, D:2 * D], znT[:, :], start=True, stop=True).then_inc(S("k"), 1)

                def w_t():
                    wait(pe, "w", g, 1, 1)
                    pe.transpose(b7[0:TT * E, 0:P], rt[:, 5, :, :].rearrange("p t e -> p (t e)"), ident[:, :])\
                        .then_inc(S("wt"), 1)

                def v():
                    wait(pe, "wT", g, 1, 1)
                    for t in range(TT):
                        m = pe.matmul(b7[:, t * P:(t + 1) * P], znT[:, t * P:(t + 1) * P], wqkv_sb[:, 2 * D:3 * D],
                                      start=True, stop=True)
                    m.then_inc(S("v"), 1)
                return {8: [t1], 11: [logits], 17: [t2], 20: [qk], 22: [w_t], 26: [v]}

            def experts(g):
                def up(i):
                    def step():
                        if i == 0:
                            wait(pe, "xl", g, 1, 1)
                        if isinstance(g, int) and g == 0 and i % HC == 0:
                            n = 2 * (i // HC) + 2
                            pe.wait_ge(S("w_lo_v" if n <= RAW else "w_lo_p"), n if n <= RAW else n - RAW)
                        wait(pe, "h32", g, HT, i - 1)
                        e, c = i // HC, i % HC
                        o = bank[i % 2][:, :]
                        ws = slice(c * P, (c + 1) * P)
                        pe.matmul(o, w1h[:, e, ws], G(xh, g), start=True, stop=False)
                        pe.matmul(o, w1l[:, e, ws], G(xh, g), start=False, stop=False)
                        pe.matmul(o, w1h[:, e, ws], G(xl, g), start=False, stop=True).then_inc(S("h"), 1)
                    return step

                def down(i):
                    def step():
                        e, c = i // HC, i % HC
                        if c == 0:
                            wait(pe, "stt", g, E, e - 1)
                        o = bank[2 + e % 2][:, :]
                        ws = slice(c * D, (c + 1) * D)
                        wait(pe, "hh", g, HT, i + 1)
                        pe.matmul(o, w2h[:, e, ws], hh[:, i % 4, :], start=(c == 0), stop=False)
                        pe.matmul(o, w2l[:, e, ws], hh[:, i % 4, :], start=False, stop=False)
                        wait(pe, "hl", g, HT, i + 1)
                        pe.matmul(o, w2h[:, e, ws], hl[:, i % 4, :], start=False, stop=(c == HC - 1))\
                            .then_inc(S("m2"), 1)
                    return step
                plan = {i: [up(i)] for i in range(HT)}
                for i in range(HT):
                    plan.setdefault(i + 2, []).append(down(i))
                return plan

            def max_scores(it, u, t, early=False):
                if t == 0:
                    wait(pe, f"st{u}", it, 96, 96)
                wait(pe, "R", it, HB * NT, u * NT + t - (not early))
                first = 4 if early else 2 + 2 * (t % 2)
                for c in range(2):
                    m = pe.matmul(bank[first + c][:, :], q_st[0:QROWS, u, t * P:(t + 1) * P],
                                  k_st[0:QROWS, u, c * TG:(c + 1) * TG], start=True, stop=True)
                m.then_inc(S("M"), 1)

            def ring_free(it, u, what):
                at = RING.index(what) - len(ring)
                n = it * HB + u if isinstance(it, int) else None
                if n is not None:
                    skipped = {("os", 0)} if n == 0 else {("mTc", 0)} if n == NHEAD - 1 else ()
                    while at >= 0 and RING[at] in skipped:
                        at -= len(ring)
                name, i = RING[at]
                u -= at < 0
                if name == "P":
                    wait(pe, "P", it, HB * 2 * KT, u * 2 * KT + i + 1)
                elif name == "mTc":
                    wait(pe, "mTc", it, HB, u + 2)
                else:
                    wait(pe, "os", it, HB, u)

            def m_t(it, u, early=False):
                wait(pe, "nmp", it, HB, u + 1)
                if not early:
                    ring_free(it, u - 1, ("mTc", 0))
                m_tr = (b7 if early else ring_bank("mTc"))[0:PARTS * NT, 0:P // 2].bitcast(BF16)
                pe.transpose(m_tr, nmp[:, u, :, :].rearrange("p i t -> p (i t)"), ident_b[:, :])\
                    .then_inc(S("mT"), 1)

            def early(u, t):
                return lambda: max_scores(0, u, t, early=True)

            beside = {2 * n + 1: [early(n // NT, n % NT)] for n in range(2 * NT)}
            beside[19].append(lambda: m_t(0, 0, early=True))
            run_slots(range(HT), (pre(0), 0))
            expert_phase(pe, experts, pre, extra=beside)

            def scores(it, u, i):
                kt, a = i // 2, i % 2
                ring_free(it, u, ("P", i))
                pe.matmul(ring_bank("P", i)[:, :], k_st[0:SROWS, u, kt * P:(kt + 1) * P],
                          q_st[0:SROWS, u, a * TG:(a + 1) * TG], start=True, stop=True).then_inc(S("S"), 1)

            def pv(it, u, m):
                if m == 0:
                    wait(pe, "vst", it, HB, u + 1)
                    wait(pe, "oe", it, HB, u)
                wait(pe, "P", it, HB * 2 * KT, u * 2 * KT + 4 * m + 4)
                for g4 in range(4):
                    kt, a = 2 * m + g4 // 2, g4 % 2
                    mm = pe.matmul(b6[VC * g4:VC * (g4 + 1), :], v_st[:, u, kt, :],
                                   p_sb[:, kt % 4, a * TG:(a + 1) * TG],
                                   start=(m == 0), stop=(m == KT // 2 - 1), skip_group_check=True)
                mm.then_inc(S("PV"), 1)

            def o_t(it, u, final=False):
                wait(pe, "oe", it, HB, u + 1)
                if final:
                    wait(pe, "P", it, HB * 2 * KT, HB * 2 * KT)
                else:
                    ring_free(it, u + 1, ("os", 0))
                for j in range(TT):
                    m = pe.transpose(ring_bank("os")[:, j * P:(j + 1) * P], o_sb[:, u % 2, j * P:(j + 1) * P], ident[:, :])
                m.then_inc(S("ot"), 1)

            def att(it, first, last):
                for u in range(HB):
                    prev = (it, u - 1) if u else (it - 1, HB - 1)
                    has_prev = not (first and u == 0)
                    wait(pe, f"m_ld{u}", it, 16, 16)
                    for j in range(KT // 2):
                        def heads_max(t):
                            if u + 2 < HB:
                                max_scores(it, u + 2, t)
                            elif not last:
                                max_scores(it + 1, u + 2 - HB, t)
                        scores(it, u, 4 * j)
                        heads_max(2 * j)
                        if j == 1:
                            if u + 1 < HB:
                                m_t(it, u + 1)
                            elif not last:
                                m_t(it + 1, 0)
                        if j == 2 and has_prev:
                            o_t(*prev)
                        scores(it, u, 4 * j + 1)
                        if j:
                            pv(it, u, j - 1)
                        elif has_prev:
                            pv(*prev, KT // 2 - 1)
                        scores(it, u, 4 * j + 2)
                        heads_max(2 * j + 1)
                        scores(it, u, 4 * j + 3)

            pe.wait_ge(S("stt"), NG * E)
            pe.wait_ge(S("h32"), NG * HT)
            pe.wait_ge(S("kf"), NG)
            pe.wait_ge(S("vd"), NG)
            pe.wait_ge(S("R"), 2 * NT)
            pe.wait_ge(S("mTc"), 1)
            att(0, True, False)
            with pe.Fori(1, NIT - 1) as it:
                att(it, False, False)
            att(NIT - 1, False, True)
            pv(NIT - 1, HB - 1, KT // 2 - 1)
            o_t(NIT - 1, HB - 1, final=True)

            def msa_turn(g):
                wait(pe, "tmc", 0, 0, g - 1)
                for t in range(TT):
                    m = pe.transpose(bank[g % 2][:, t * P:(t + 1) * P], msa[:, g * TT + t, :], ident[:, :])
                m.then_inc(S("tm"), 1)

            def project(g):
                if g == 0:
                    pe.wait_ge(S("wp"), 16)
                wait(pe, "tmc", 0, 0, g + 1)
                wait(pe, "y", 0, 0, g - 1)
                pe.matmul(bank[2 + g % 2][:, :], wp_sb[:, :], msaT[:, g % 2, :], start=True, stop=True)\
                    .then_inc(S("tp"), 1)

            def y_turn(g):
                wait(pe, "yg", 0, 0, g + 1)
                wait(pe, "ty", 0, 0, g - 1)
                for t in range(TT):
                    m = pe.transpose(bank[4 + g % 2][:, t * P:(t + 1) * P], y2[:, g % 2, t * P:(t + 1) * P],
                                     ident[:, :])
                m.then_inc(S("tt"), 1)

            pe.wait_ge(S("msa"), NHEAD)
            for g in range(NG + 2):
                if g < NG:
                    msa_turn(g)
                if 1 <= g <= NG:
                    project(g - 1)
                if g >= 2:
                    y_turn(g - 2)

        @block.vector
        def _(dve):
            dve.memset(q_st[64:P, :, :], 0.0).then_inc(S("zeros"), 1)
            dve.memset(k_st[64:QROWS, :, :], 0.0).then_inc(S("zeros"), 1)
            dve.memset(k_st[QROWS:P, :, :], 1.0).then_inc(S("zeros"), 1)
            dve.memset(zero8[:, :], 0.0).then_inc(S("zeros"), 1)
            ch = Chain(dve, S("dve"))

            def guess_rsqrt(k):
                def step():
                    v, y, hv = (nwt[:, i, :] for i in range(3))
                    ch.mark(dve.tensor_scalar(v, mv[:, :, 1], EPS, None, ALU.add))
                    ch.sync()
                    ch.mark(dve.tensor_scalar(guess[:, :], v.bitcast(I32), 1, None, ALU.logical_shift_right))
                    ch.mark(dve.tensor_scalar(hv, v, -0.5, None, ALU.mult))
                    ch.sync()
                    dve.tensor_scalar(y.bitcast(I32), guess[:, :], -1.0, float(RSQRT_GUESS), ALU.mult, ALU.add)\
                        .then_inc(S("guess"), 1)
                return step

            def spread(t0, t1):
                def step():
                    for t in range(t0, t1):
                        i = dve.bn_stats(st1[:, t, :], xz[:, t, :])
                    ch.mark(i)
                return step

            def moments():
                ch.sync()
                for t in range(TT):
                    i = dve.bn_aggr(mv[:, t, :], st1[:, t, :])
                ch.mark(i)
                ch.sync()

            def pre(g):
                def x_here():
                    wait(dve, "x", g, 16, 16)

                def z_here():
                    wait(dve, "xn", g, 1, 1)

                def normalise(done):
                    def step():
                        wait(dve, "nwt", g, 2, 1 if done == "xn" else 2)
                        if done == "zn":
                            wait(dve, "t1", g, 1, 1)
                        for t in range(TT):
                            i = dve.tensor_scalar(xz[:, t, :], xz[:, t, :], mv[:, t, 0:1], nwt[:, 1, t:t + 1],
                                                  ALU.subtract, ALU.mult)
                        i.then_inc(S(done), 1)
                    return step

                def high_x():
                    wait(dve, "xnT", g, 1, 1)
                    dve.tensor_copy(G(xh, g), xnT[:, :]).then_inc(S("xh"), 1)

                def low_x():
                    wait(dve, "xh", g, 1, 1)
                    dve.tensor_tensor(G(xl, g), xnT[:, :], G(xh, g).bitcast(F32), ALU.subtract)\
                        .then_inc(S("xl"), 1)

                def router_top():
                    wait(dve, "lg", g, 1, 1)
                    ch.mark(dve.tensor_tensor(lg[:, :, :], b7[:, 0:TT * E].rearrange("p (t e) -> p t e", e=E),
                                              br_bc[:, :].unsqueeze(1).broadcast_to([P, TT, E]), ALU.add))
                    ch.sync()
                    for t in range(TT):
                        i = dve.max(top[:, t, :], lg[:, t, :])
                    ch.mark(i)
                    ch.sync()
                    dve.tensor_tensor(rt[:, 0, :, :], lg[:, :, :], top[:, :, 0:1].broadcast_to([P, TT, E]),
                                      ALU.subtract).then_inc(S("dlt"), 1)
                    ch.mark(dve.tensor_tensor(rt[:, 2, :, :], lg[:, :, :], top[:, :, 1:2].broadcast_to([P, TT, E]),
                                              ALU.is_ge))

                def router_weights():
                    wait(dve, "th", g, 1, 1)
                    ch.mark(dve.tensor_scalar(rt[:, 3, :, :], rt[:, 1, :, :], 1.0, None, ALU.add))
                    ch.mark(dve.tensor_scalar(rt[:, 4, :, :], rt[:, 1, :, :], -1.0, 1.0, ALU.mult, ALU.add))
                    ch.sync()
                    ch.mark(dve.reciprocal(rt[:, 4, :, :], rt[:, 4, :, :]))
                    ch.sync()
                    ch.mark(dve.tensor_tensor(rt[:, 3, :, :], rt[:, 3, :, :], rt[:, 4, :, :], ALU.mult))

                def router_sum():
                    ch.sync()
                    ch.mark(dve.tensor_tensor(rt[:, 3, :, :], rt[:, 3, :, :], rt[:, 2, :, :], ALU.mult))
                    ch.sync()
                    ch.mark(dve.tensor_reduce(rs[:, 0, :], rt[:, 3, :, :], AX.X, ALU.add))
                    ch.sync()
                    ch.mark(dve.reciprocal(rs[:, 1, :], rs[:, 0, :]))

                def router_done():
                    ch.end()
                    wait(dve, "wt", g, 1, 0)
                    dve.tensor_tensor(rt[:, 5, :, :], rt[:, 3, :, :],
                                      rs[:, 1, :].unsqueeze(2).broadcast_to([P, TT, E]), ALU.mult)\
                        .then_inc(S("w"), 1)

                def first(w):
                    def step():
                        wait(dve, ("qf", "kf")[w], g, 1, 1)
                        wait(dve, "qp_st", g, QP_ST, 0)
                        dve.tensor_copy(qkp[:, w, 0, :], qkf[:, w, :]).then_inc(S("p0"), 1)
                    return step

                def second(w):
                    def step():
                        wait(dve, "r1", g, 2, w + 1)
                        dve.tensor_copy(qkp[:, w, 1, :], qkf[:, w, :]).then_inc(S("p1"), 1)
                    return step

                def values():
                    wait(dve, "v", g, 1, 1)
                    dst = v_sb[:, g * TT:(g + 1) * TT, :] if isinstance(g, int) else v_sb[:, bass.ds(g * TT, TT), :]
                    dve.tensor_tensor(dst, b7[:, :].rearrange("p (t d) -> p t d", d=D),
                                      bv_bc[:, :].unsqueeze(1).broadcast_to([P, TT, D]), ALU.add)\
                        .then_inc(S("vd"), 1)
                return {0: [x_here, spread(0, 2)], 1: [spread(2, 4)], 2: [moments], 3: [guess_rsqrt(1)],
                        7: [normalise("xn")], 8: [z_here, spread(0, 2)], 9: [spread(2, 4)], 10: [moments],
                        11: [guess_rsqrt(2), high_x], 12: [low_x], 14: [router_top], 15: [normalise("zn")],
                        17: [router_weights], 18: [router_sum], 19: [router_done],
                        22: [first(0)], 23: [first(1)], 26: [second(0)], 27: [second(1)], 29: [values]}

            def experts(g):
                def low_h(i):
                    def step():
                        wait(dve, "h32", g, HT, i + 1)
                        wait(dve, "m2", g, HT, i - 3)
                        dve.tensor_tensor(hl[:, i % 4, :], h32[:, i % 2, :], hh[:, i % 4, :].bitcast(F32),
                                          ALU.subtract).then_inc(S("hl"), 1)
                    return step

                def combine(e):
                    def step():
                        wait(dve, "m2", g, HT, (e + 1) * HC)
                        if isinstance(g, int):
                            dve.wait_ge(s_wbc[e], 16 * (g + 1))
                        else:
                            dve.wait_ge(s_wbc[e], 16 * g + 16)
                        if e == 0:
                            wait(dve, "acc", g, E - 1, 0)
                        if e > 2:
                            wait(dve, "acc", g, E - 1, e - 2)
                        dst = prod[:, e % 2, :] if e else acc[:, :]
                        dve.scalar_tensor_tensor(dst, bank[2 + e % 2][:, :], col(C_B2 + e), wbc[:, e, :],
                                                 ALU.add, ALU.mult).then_inc(S("stt"), 1)
                    return step
                def total():
                    wait(dve, "stt", g, E, E)
                    wait(dve, "acc", g, E - 1, E - 2)
                    dve.tensor_tensor(G(ffn, g), acc[:, :], prod[:, (E - 1) % 2, :], ALU.add).then_inc(S("acc"), 1)

                plan = {4 * e + 6: [combine(e)] for e in range(E)}
                plan[4 * E + 4] = [total]
                for i in range(HT):
                    plan.setdefault(i, []).append(low_h(i))
                return plan

            def row_max(it, u, t, early=False):
                wait(dve, "M", it, HB * NT, u * NT + t + 1)
                pair = psum[:, 4 * TG:6 * TG] if early else wide_banks[t % 2]
                dve.tensor_reduce(mx[:, u, t:t + 1], pair, AX.X, ALU.max, negate=True).then_inc(S("R"), 1)

            def lo(ns):
                return [lambda n=n: weights_lo(dve, n) for n in ns]

            def early(u, t):
                return lambda: row_max(0, u, t, early=True)

            run_slots(range(HT), (pre(0), 0), ({12: lo(range(2)), 14: lo([2]), 17: lo([3]), 21: lo(range(4, RAW))}, 0))
            expert_phase(dve, experts, pre, extra={2 * n + 2: [early(n // NT, n % NT)] for n in range(2 * NT)})

            def head_out(it, u):
                wait(dve, "ot", it, HB, u + 1)
                turned = ring_bank("os")[:, :].rearrange("p (j k a r) -> p a j r k", k=2, a=2, r=VC)
                for a in range(2):
                    i = dve.tensor_reduce(o9[:, u % 2, a * TT:(a + 1) * TT, :], turned[:, a, :, 0:DH + 1, :],
                                          AX.X, ALU.add)
                i.then_inc(S("os"), 1)
                wait(dve, "os", it, HB, u + 1)
                dve.reciprocal(rden[:, u % 2, :], o9[:, u % 2, :, DH]).then_inc(S("rd"), 1)
                wait(dve, "rd", it, HB, u + 1)
                b, h = it // (H // HB), (it % (H // HB)) * HB + u
                dst = msa[:, b * NT:(b + 1) * NT, h * DH:(h + 1) * DH] if isinstance(it, int) else \
                    msa[:, bass.ds(b * NT, NT), bass.ds(h * DH, DH)]
                dve.tensor_tensor(dst, o9[:, u % 2, :, 0:DH], rden[:, u % 2, :].unsqueeze(2)
                                  .broadcast_to([P, NT, DH]), ALU.mult).then_inc(S("msa"), 1)

            def att(it, first, last):
                for u in range(HB):
                    for t in range(NT):
                        m = u + 2
                        if m < HB:
                            row_max(it, m, t)
                        elif not last:
                            row_max(it + 1, m - HB, t)
                        if t == 4 and not (first and u == 0):
                            head_out(*((it, u - 1) if u else (it - 1, HB - 1)))

            att(0, True, False)
            with dve.Fori(1, NIT - 1) as it:
                att(it, False, False)
            att(NIT - 1, False, True)
            head_out(NIT - 1, HB - 1)


            def gated(g):
                k = g % 2
                wait(dve, "tp", 0, 0, g + 1)
                dve.scalar_tensor_tensor(y1[:, k, :], bank[2 + k][:, :], col(C_BP), xh[:, g, :].bitcast(F32),
                                         ALU.add, ALU.add).then_inc(S("y"), 1)
                wait(dve, "y", 0, 0, g + 1)
                wait(dve, "tt", 0, 0, g - 1)
                dve.tensor_tensor(y2[:, k, :], y1[:, k, :], xl[:, g, :].bitcast(F32), ALU.add).then_inc(S("ya"), 1)
                wait(dve, "ya", 0, 0, g + 1)
                wait(dve, "gate", 0, 0, g + 1)
                dve.tensor_tensor(y2[:, k, :], y2[:, k, :], ffn[:, g, :], ALU.mult).then_inc(S("yg"), 1)

            def finish(g):
                k = g % 2
                wait(dve, "tt", 0, 0, g + 1)
                wait(dve, f"tx{k}", 0, 0, 16 * (g // 2 + 1))
                dst = x_out[:, k, :, :]
                dve.tensor_tensor(dst, bank[4 + k][:, :].rearrange("p (t d) -> p t d", d=D), dst, ALU.add)\
                    .then_inc(S("ty"), 1)
            for g in range(NG + 1):
                if g < NG:
                    gated(g)
                if g:
                    finish(g - 1)


_INS = ["L0_attn_z", "L0_attn_ln_w", "L0_attn_ln_b", "L0_attn_W_qkv", "L0_attn_b_qkv", "L0_attn_W_proj",
        "L0_attn_b_proj", "L0_ffn_W1", "L0_ffn_b1", "L0_ffn_W2", "L0_ffn_b2", "L0_ffn_Wr", "L0_ffn_br"]


def kernel(**inputs):
    import numpy as _np
    import concourse.bacc as _bacc
    from concourse import mybir as _mybir
    from concourse.bass_utils import run_bass_kernel_spmd as _run

    nc = _bacc.Bacc("TRN2", target_bir_lowering=False, num_devices=1)
    arrays, args = {}, []
    for name in _INS:
        a = _np.ascontiguousarray(inputs[name])
        arrays[f"in_{name}_dram"] = a
        args.append(nc.dram_tensor(f"in_{name}_dram", a.shape, _mybir.dt.from_np(a.dtype), kind="ExternalInput").ap())
    shape = inputs["L0_attn_z"].shape
    args.append(nc.dram_tensor("out_0_dram", shape, _mybir.dt.float32, kind="ExternalOutput").ap())
    attention_and_experts(nc, *args)
    r = _run(nc, [arrays], core_ids=[0])
    return r.results[0]["out_0_dram"]
```

```python
from contextlib import ExitStack

import concourse.bass as bass
from concourse import mybir

ALU = mybir.AluOpType
ACT = mybir.ActivationFunctionType
AX = mybir.AxisListType
F32 = mybir.dt.float32
F32R = mybir.dt.float32r
BF16 = mybir.dt.bfloat16
I32 = mybir.dt.int32

P = 128
TG = 512
TT = TG // P
PARTS = 3
QROWS = 96
SROWS = QROWS + PARTS
VC = 32
EPS = 1e-5
RSQRT_GUESS = 0x5F3759DF
NEWTON = 3


class Chain:

    def __init__(self, eng, sem):
        self.eng, self.sem, self.n = eng, sem, 0

    def mark(self, ins):
        self.n += 1
        ins.then_inc(self.sem, 1)

    def sync(self):
        self.eng.wait_ge(self.sem, self.n)

    def end(self):
        self.sync()
        self.eng.sem_inc(self.sem, -self.n)
        self.n = 0


def run_slots(slots, *plans):
    for s in slots:
        for plan, shift in plans:
            for step in plan.get(s + shift, []):
                step()


def attention_and_experts(nc, x, ln_w, ln_b, w_qkv, b_qkv, w_proj, b_proj, w1, b1, w2, b2, w_r, b_r, out):
    B, N, D = x.shape
    E, _, HID = w1.shape
    H = 16
    DH = D // H
    SCALE = float(DH) ** -0.5
    NG = B * N // TG
    HC = HID // P
    HT = E * HC
    KT = N // P
    NT = N // P
    NHEAD = B * H
    HB = 4
    RAW = 8
    NIT = NHEAD // HB
    LAG = 6
    assert D == P and N % TG == 0 and N // TG == 2 and HID % P == 0

    x_g = x.rearrange("b (g t p) d -> (b g) p t d", p=P, t=TT)
    out_g = out.rearrange("b (g t p) d -> (b g) p t d", p=P, t=TT)

    q_dram = nc.dram_tensor("q_parts_dram", (B, D, PARTS, N), BF16, kind="Internal").ap()
    k_dram = nc.dram_tensor("k_parts_dram", (PARTS, B, D, PARTS, N), BF16, kind="Internal").ap()
    w_dram = nc.dram_tensor("expert_w_dram", (NG, TT, E, P), F32, kind="Internal").ap()
    m_dram = nc.dram_tensor("neg_max_dram", (HB, PARTS * NT, P), BF16, kind="Internal").ap()
    q_rows = q_dram.rearrange("b r i t -> (b r i) t")
    k_rows = k_dram.rearrange("j b r i t -> j (b r i) t")

    with ExitStack() as ctx:
        def sb(name, shape, dt=F32, c=ctx):
            return c.enter_context(nc.sbuf_tensor(name, shape, dt))

        def sem(name):
            return ctx.enter_context(nc.semaphore(name))

        xh = sb("xn_t_hi", [P, NG, TG], F32R)
        xl = sb("xn_t_lo", [P, NG, TG], F32R)
        ffn = sb("ffn_t", [P, NG, TG])
        v_sb = sb("v_sb", [P, B * KT, D])
        q_st = sb("q_stack", [P, HB, N], BF16)
        k_st = sb("k_stack", [P, HB, N], BF16)
        ident = sb("ident", [P, P])
        ident_b = sb("ident_b", [P, P], BF16)
        cols = sb("cols", [P, 64])
        zero8 = sb("zero8", [P, NT])

        mx = sb("neg_max", [P, HB, NT])
        nm = sb("neg_max_rest", [P, HB, NT])
        nmp = sb("neg_max_parts", [P, HB, PARTS, NT], BF16)

        ffn_ctx = ExitStack()
        fs = lambda name, shape, dt=F32: sb(name, shape, dt, ffn_ctx)
        w1h = fs("w1_hi", [P, E, HID], F32R)
        w1l = fs("w1_lo", [P, E, HID], F32R)
        w2h = fs("w2_hi", [P, E, HC * D], F32R)
        w2l = fs("w2_lo", [P, E, HC * D], F32R)
        wbc = fs("expert_w_bc", [P, E, TG])
        hh = fs("h_hi", [P, 4, TG], F32R)
        hl = fs("h_lo", [P, 4, TG], F32R)
        h32 = fs("h_full", [P, 2, TG])
        prod = fs("prod", [P, 2, TG])
        acc = fs("acc", [P, TG])
        xz = fs("xz", [P, TT, D])
        xnT = fs("xn_t", [P, TG])
        znT = fs("zn_t", [P, TG])
        qkf = fs("qk_full", [P, 2, TG])
        qkp = fs("qk_parts", [P, 2, PARTS, TG], BF16)
        wqkv_sb = fs("wqkv_sb", [P, 3 * D])
        wr_sb = fs("wr_sb", [P, E])
        bv_bc = fs("bv_bc", [P, D])
        br_bc = fs("br_bc", [P, E])
        st1 = fs("bn_parts", [P, TT, 6])
        mv = fs("mean_var", [P, TT, 2])
        nwt = fs("newton", [P, 4, TT])
        guess = fs("guess", [P, TT], I32)
        lg = fs("logits", [P, TT, E])
        top = fs("top8", [P, TT, 8])
        rt = fs("router", [P, 6, TT, E])
        rs = fs("router_sum", [P, 2, TT])
        wT = fs("w_t", [TT * E, P])
        rows = acc[0:48, 0:P]
        nmT = wT[0:PARTS * NT, :].bitcast(BF16).rearrange("k (s p) -> k s p", s=2)
        ffn_ctx.close()
        w_raw = ffn

        att_ctx = ExitStack()
        ats = lambda name, shape, dt=F32: sb(name, shape, dt, att_ctx)
        p_sb = ats("p_ring", [P, 4, N])
        v_st = ats("v_stack", [P, HB, KT, VC])
        wp_sb = ats("wp_sb", [P, D])
        o_sb = ats("o_sb", [P, 2, TG])
        o9 = ats("o_sum", [P, 2, NT, DH + 1])
        rden = ats("rden", [P, 2, NT])
        msa = ats("msa", [P, B * NT, D])
        msaT = ats("msa_t", [P, 2, TG])
        y = ats("y", [P, NG, TG])
        x_out = ats("x_out", [P, NG, TT, D])
        att_ctx.close()

        psum = ctx.enter_context(nc.psum_tensor("psum", [P, 8 * TG], F32))
        bank = [psum[:, i * TG:(i + 1) * TG] for i in range(8)]
        wide_banks = [psum[:, (2 + 2 * i) * TG:(4 + 2 * i) * TG] for i in range(2)]
        b5, b6, b7 = bank[5], bank[6], bank[7]
        ring = [bank[0], bank[1], bank[7]]
        RING = [("P", i) for i in range(2 * KT)]
        RING.insert(RING.index(("P", 6)), ("mTc", 0))
        RING.insert(RING.index(("P", 9)), ("os", 0))
        assert len(RING) % len(ring) == 0

        def ring_bank(name, i=0):
            return ring[RING.index((name, i)) % len(ring)]

        C_B1, C_B2 = 0, HT
        C_LNW, C_LNB, C_BQ, C_BK, C_BP = (HT + E + i for i in range(5))
        NROW = HT + E + 5

        BESIDE = NG - NG // B
        POOL_GATES = range(2 * BESIDE // 3)
        DVE_GATES = [g for g in range(NG) if g not in POOL_GATES]

        def col(i):
            return cols[:, i:i + 1]

        sems = {}

        def S(name):
            if name not in sems:
                sems[name] = sem("s_" + name)
            return sems[name]

        s_wbc = [sem(f"s_wbc{e}") for e in range(E)]

        def wait(eng, name, it, per, k):
            if isinstance(it, int):
                if it * per + k > 0:
                    eng.wait_ge(S(name), it * per + k)
            else:
                eng.wait_ge(S(name), it * per + k)

        def weights_lo(eng, n):
            e, slot = n // 2, n % RAW
            hi, lo = ((w1h, w1l), (w2h, w2l))[n % 2]
            eng.wait_ge(S("w_hi"), n + 1)
            eng.tensor_tensor(lo[:, e, :], w_raw[:, slot, :], hi[:, e, :].bitcast(F32), ALU.subtract)\
                .then_inc(S("w_lo_v" if n < RAW else "w_lo_p"), 1)

        def G(t, g):
            return t[:, g, :] if isinstance(g, int) else t[:, bass.ds(g, 1), :].rearrange("p a t -> p (a t)")

        block = ctx.enter_context(nc.Block())

        AHEAD = {13: 0, 14: 1, 17: 2, 22: 3}
        AHEAD_V = {15: 0, 16: 1, 20: 2, 22: 3}

        def prepare_first(pre, experts, extra=None, ahead=AHEAD):
            run_slots(range(HT), (pre(0), 0), (extra or {}, 0),
                      ({at: experts(0).get(k, []) for at, k in ahead.items()}, 0))

        def expert_phase(eng, experts, pre, first=None, extra=None):
            full = range(HT)

            def body(g, carry=True):
                plans = [(pre(g + 1), 0), (experts(g), 0)]
                if isinstance(g, int) and g == 0:
                    plans = [(first or {}, 0), plans[0],
                             ({k: steps for k, steps in experts(0).items() if k not in AHEAD.values()}, 0)]
                if carry:
                    plans.insert(0, (experts(g - 1), HT))
                run_slots(full, *plans)
            body(0, carry=False)
            with eng.Fori(1, NG - 1) as g:
                body(g)
            last = NG - 1
            run_slots(full, (experts(last - 1), HT), (extra or {}, 0), (experts(last), 0))
            run_slots(range(LAG), (extra or {}, HT), (experts(last), HT))

        QP_ST = 6 * 16

        def sp_weight(sp, n):
            e, slot = n // 2, n % RAW
            if n >= RAW:
                sp.wait_ge(S("w_lo_v"), n - RAW + 1)
            dst = w_raw[:, slot, :]
            if n % 2 == 0:
                sp.dma_start(dst, w1[e, :, :]).then_inc(S(f"w_raw{slot}"), 16)
            else:
                sp.dma_start(dst.rearrange("p (c d) -> p c d", c=HC),
                             w2[e, :, :].rearrange("(c p) d -> p c d", p=P)).then_inc(S(f"w_raw{slot}"), 16)

        def sp_load_x(sp, g):
            wait(sp, "t2", g, 1, 0)
            src = x_g[g] if isinstance(g, int) else x_g[bass.ds(g, 1)].rearrange("a p t d -> (a p) t d")
            sp.dma_start(xz[:, :, :], src).then_inc(S("x"), 16)

        def sp_store_w(sp, g):
            wait(sp, "wT", g, 1, 1)
            dst = w_dram[g] if isinstance(g, int) else w_dram[bass.ds(g, 1)].rearrange("a t e p -> (a t) e p")
            sp.dma_start(dst.rearrange("t e p -> (t e) p"), wT[:, :]).then_inc(S("w_st"), 16)

        def sp_store_qk(sp, g):
            b, half = g // 2, g % 2
            tokens = slice(half * TG, (half + 1) * TG) if isinstance(g, int) else bass.ds(half * TG, TG)

            def batch(t):
                return t[b] if isinstance(g, int) else t[bass.ds(b, 1)].rearrange("a r i t -> (a r) i t")
            wait(sp, "qp", g, 2, 1)
            sp.dma_start(batch(q_dram)[:, :, tokens], qkp[:, 0, :, :]).then_inc(S("qp_st"), 16)
            wait(sp, "qp", g, 2, 2)
            for j in range(PARTS):
                dst = batch(k_dram[j])[:, :, tokens]
                sp.dma_start(dst[:, 0:PARTS - j, :], qkp[:, 1, j:PARTS, :]).then_inc(S("qp_st"), 16)
                if j:
                    sp.dma_start(dst[:, PARTS - j:PARTS, :], qkp[:, 1, 0:j, :]).then_inc(S("qp_st"), 16)

        def sp_wbc(sp, g, e):
            if e == 0:
                wait(sp, "w_st", g, 16, 16)
            wait(sp, "stt", g, E, e + 1 - E)
            src = w_dram[g, :, e, :] if isinstance(g, int) else \
                w_dram[bass.ds(g, 1), :, e, :].rearrange("a t p -> (a t) p")
            sp.dma_start(wbc[:, e, :].rearrange("p (t c) -> p t c", t=TT), src.partition_broadcast(P))\
                .then_inc(s_wbc[e], 16)

        def sp_stage(sp, n, u):
            r0 = n * (DH * PARTS)

            def rows_of(t):
                return t[r0:r0 + DH * PARTS, :] if isinstance(n, int) else t[bass.ds(r0, DH * PARTS), :]
            for j in range(PARTS):
                lo = j * DH * PARTS
                sp.dma_start(q_st[lo:lo + DH * PARTS, u, :], rows_of(q_rows)).then_inc(S(f"st{u}"), 16)
                sp.dma_start(k_st[lo:lo + DH * PARTS, u, :], rows_of(k_rows[j])).then_inc(S(f"st{u}"), 16)

        def sp_att(sp, it, last):
            for u in range(HB):
                m = u + 1
                if not (last and m >= HB):
                    slot, mit = m % HB, it + m // HB
                    wait(sp, "mTc", mit, HB, slot + 1)
                    sp.dma_start(m_dram[slot], nmT[:, slot % 2, :]).then_inc(S("m_st"), 16)
                    wait(sp, "m_st", mit, HB * 16, (slot + 1) * 16)
                    sp.dma_start(q_st[QROWS:SROWS, slot, :],
                                 m_dram[slot].rearrange("(i t) c -> i (t c)", i=PARTS)).then_inc(S(f"m_ld{slot}"), 16)
                if not last:
                    wait(sp, "S", it, HB * 2 * KT, (u + 1) * 2 * KT)
                    sp_stage(sp, (it + 1) * HB + u, u)

        @block.sync
        def _(sp):
            sp_load_x(sp, 0)
            for r0, r1, src in ((0, HT, b1.rearrange("e (c p) -> (e c) p", p=P)), (HT, HT + E, b2),
                                (C_LNW, C_LNW + 1, ln_w.rearrange("(a p) -> a p", a=1)),
                                (C_LNB, C_LNB + 1, ln_b.rearrange("(a p) -> a p", a=1)),
                                (C_BQ, C_BQ + 2, b_qkv[0:2 * D].rearrange("(a p) -> a p", p=P)),
                                (C_BP, C_BP + 1, b_proj.rearrange("(a p) -> a p", a=1))):
                sp.dma_start(rows[r0:r1, :], src).then_inc(S("rows"), 16)
            sp.dma_start(wqkv_sb[:, :], w_qkv).then_inc(S("const"), 16)
            sp.dma_start(wr_sb[:, :], w_r).then_inc(S("const"), 16)
            sp.dma_start(bv_bc[:, :], b_qkv[2 * D:3 * D].partition_broadcast(P)).then_inc(S("const"), 16)
            sp.dma_start(br_bc[:, :], b_r.partition_broadcast(P)).then_inc(S("const"), 16)
            for n in range(RAW):
                sp_weight(sp, n)
            sp_load_x(sp, 1)

            def spread_w(g):
                for e in range(E):
                    sp_wbc(sp, g, e)

            for n in range(RAW, RAW + 3):
                sp_weight(sp, n)
            sp_store_w(sp, 0)
            spread_w(0)
            for n in range(RAW + 3, 2 * E):
                sp_weight(sp, n)
            sp_store_qk(sp, 0)

            def body(g, more=True):
                sp_store_w(sp, g)
                sp_store_qk(sp, g)
                if more:
                    sp_load_x(sp, g + 1)
                spread_w(g)

            with sp.Fori(1, NG - 1) as g:
                body(g)
            sp.wait_ge(S("zeros"), 3)
            sp.wait_ge(S("qp_st"), (NG - 1) * QP_ST)
            for u in range(HB):
                sp_stage(sp, u, u)
            body(NG - 1, more=False)
            sp.wait_ge(S("qp_st"), NG * QP_ST)
            sp.wait_ge(S("mTc"), 1)
            sp.dma_start(m_dram[0], nmT[:, 0, :]).then_inc(S("m_st"), 16)
            sp.wait_ge(S("m_st"), 16)
            sp.dma_start(q_st[QROWS:SROWS, 0, :], m_dram[0].rearrange("(i t) c -> i (t c)", i=PARTS))\
                .then_inc(S("m_ld0"), 16)
            sp.wait_ge(S("m2"), NG * HT)
            sp.wait_ge(S("acc"), NG * (E - 1))
            sp.dma_start(wp_sb[:, :], w_proj).then_inc(S("wp"), 16)
            for g in range(NG):
                sp.dma_start(x_out[:, g, :, :], x_g[g]).then_inc(S("tx"), 16)
            sp_att(sp, 0, False)
            with sp.Fori(1, NIT - 1) as it:
                sp_att(sp, it, False)
            sp_att(sp, NIT - 1, True)

            for g in range(NG):
                wait(sp, "ty", 0, 0, g + 1)
                sp.dma_start(out_g[g], x_out[:, g, :, :]).then_inc(S("out"), 16)
            sp.wait_ge(S("out"), 16 * NG)
            sp.wait_ge(S("qp_st"), NG * QP_ST)
            sp.wait_ge(S("w_st"), NG * 16)
            sp.wait_ge(S("m_st"), NHEAD * 16)

        @block.gpsimd
        def _(pool):
            for n, t in enumerate((ident, ident_b)):
                pool.memset(t[:, :], 0.0).then_inc(S("pool"), 1)
                pool.wait_ge(S("pool"), n + 1)
                pool.affine_select(out=t[:, :], in_=t[:, :], compare_op=ALU.not_equal, fill=1.0, base=0,
                                   pattern=[[-1, P]], channel_multiplier=1).then_inc(S("ident"), 1)
            ch = Chain(pool, S("pool_own"))

            def pre(g):
                def rest(w):
                    def step():
                        wait(pool, "p0", g, 2, w + 1)
                        pool.tensor_tensor(qkf[:, w, :], qkf[:, w, :], qkp[:, w, 0, :], ALU.subtract)\
                            .then_inc(S("r1"), 1)
                    return step

                def third(w):
                    def step():
                        wait(pool, "p1", g, 2, w + 1)
                        pool.tensor_tensor(qkp[:, w, 2, :], qkf[:, w, :], qkp[:, w, 1, :], ALU.subtract)\
                            .then_inc(S("qp"), 1)
                    return step
                return {4: [newton(g, 1)], 10: [newton(g, 2)], 21: [rest(0)], 22: [rest(1)],
                        25: [third(0)], 26: [third(1)]}

            def neg_parts(it, u):
                wait(pool, "R", it, HB * NT, (u + 1) * NT)
                a, r = mx[:, u, :], nm[:, u, :]
                p = [nmp[:, u, i, :] for i in range(PARTS)]
                ch.mark(pool.tensor_tensor(p[0], a, zero8[:, :], ALU.add))
                ch.sync()
                ch.mark(pool.tensor_tensor(r, a, p[0], ALU.subtract))
                ch.sync()
                ch.mark(pool.tensor_copy(p[1], r))
                ch.end()
                pool.tensor_tensor(p[2], r, p[1], ALU.subtract).then_inc(S("nmp"), 1)

            def newton(g, k):
                def step():
                    if isinstance(g, int) and g == 0:
                        return
                    y, hv, a = (nwt[:, i, :] for i in (1, 2, 3))
                    wait(pool, "guess", g, 2, k)
                    for n in range(NEWTON):
                        ch.mark(pool.tensor_tensor(a, y, y, ALU.mult))
                        ch.sync()
                        ch.mark(pool.tensor_tensor(a, a, hv, ALU.mult))
                        ch.sync()
                        ch.mark(pool.tensor_scalar(a, a, 1.5, None, ALU.add))
                        if n < NEWTON - 1:
                            ch.sync()
                            ch.mark(pool.tensor_tensor(y, y, a, ALU.mult))
                            ch.sync()
                    ch.end()
                    pool.tensor_tensor(y, y, a, ALU.mult).then_inc(S("nwt"), 1)
                return step

            def experts(g):
                def add(e):
                    def step():
                        wait(pool, "stt", g, E, e + 1)
                        if e > 1:
                            wait(pool, "acc", g, E - 1, e - 1)
                        pool.tensor_tensor(acc[:, :], acc[:, :], prod[:, e % 2, :], ALU.add).then_inc(S("acc"), 1)
                    return step
                return {4 * e + 7: [add(e)] for e in range(1, E - 1)}

            def padding():
                pool.memset(q_st[:, :, :], 0.0).then_inc(S("zeros"), 1)
                pool.memset(k_st[:, :, :], 1.0).then_inc(S("zeros"), 1)
                pool.memset(zero8[:, :], 0.0).then_inc(S("zeros"), 1)

            prepare_first(pre, experts, {11: [padding]})
            expert_phase(pool, experts, pre,
                         first={2 * (n - RAW) + 4: [lambda n=n: weights_lo(pool, n)] for n in range(RAW, 2 * E)},
                         extra={17: [lambda: (pool.wait_ge(S("zeros"), 3), neg_parts(0, 0))], HT + 1: [lambda: neg_parts(0, 1)]})

            pool.wait_ge(S("m2"), NG * HT)
            pool.memset(v_st[:, :, :, DH + 1:VC], 0.0).then_inc(S("vinit"), 1)
            pool.memset(v_st[:, :, :, DH:DH + 1], 1.0).then_inc(S("vinit"), 1)
            def stage_v(it, u):
                b, h = it // (H // HB), (it % (H // HB)) * HB + u
                wait(pool, "PV", it, HB * KT // 2, (u + 1 - HB) * KT // 2)
                if isinstance(b, int):
                    src = v_sb[:, b * KT:(b + 1) * KT, h * DH:(h + 1) * DH]
                else:
                    src = v_sb[:, bass.ds(b * KT, KT), bass.ds(h * DH, DH)]
                pool.tensor_copy(v_st[:, u, :, 0:DH], src).then_inc(S("vst"), 1)

            def att(it, first, last):
                for u in range(HB):
                    if not (first and u == 0):
                        stage_v(it, u)
                    if first:
                        for g in range(u * NG // HB, (u + 1) * NG // HB):
                            pool.tensor_tensor(y[:, g, :], xh[:, g, :].bitcast(F32), xl[:, g, :].bitcast(F32),
                                               ALU.add).then_inc(S("xf"), 1)
                    m = u + 2
                    if m < HB:
                        neg_parts(it, m)
                    elif not last:
                        neg_parts(it + 1, m - HB)

            pool.wait_ge(S("vd"), NG)
            stage_v(0, 0)
            att(0, True, False)
            with pool.Fori(1, NIT - 1) as it:
                att(it, False, False)
            att(NIT - 1, False, True)

            for k, g in enumerate(POOL_GATES):
                wait(pool, "gate", 0, 0, g + 1)
                wait(pool, "y", 0, 0, g + 1)
                pool.tensor_tensor(y[:, g, :], y[:, g, :], ffn[:, g, :], ALU.mult).then_inc(S("yg_p"), 1)

        @block.scalar
        def _(act):
            act.wait_ge(S("cols_t"), 1)
            act.activation(cols[:, 0:NROW], b7[:, 0:NROW], ACT.Copy).then_inc(S("cols"), 1)

            def weights_hi(n):
                e, slot = n // 2, n % RAW
                hi = (w1h, w2h)[n % 2]
                act.wait_ge(S(f"w_raw{slot}"), 16 * (n // RAW + 1))
                act.activation(hi[:, e, :], w_raw[:, slot, :], ACT.Copy).then_inc(S("w_hi"), 1)

            def pre(g):
                def x_t():
                    wait(act, "t1", g, 1, 1)
                    wait(act, "xl", g, 1, 0)
                    wait(act, "lg", g, 1, 0)
                    act.activation(xnT[:, :], b5[:, :], ACT.Copy).then_inc(S("xnT"), 1)

                def z_t():
                    if isinstance(g, int) and g == 0:
                        act.wait_ge(S("cols"), 1)
                    wait(act, "t2", g, 1, 1)
                    wait(act, "v", g, 1, 0)
                    act.activation(znT[:, :], b6[:, :], ACT.Identity, scale=col(C_LNW), bias=col(C_LNB))\
                        .then_inc(S("znT"), 1)

                def qk(w):
                    def step():
                        wait(act, ("q", "k")[w], g, 1, 1)
                        wait(act, "qp", g, 2, w - 1)
                        bk, bias = ((b5, C_BQ), (b6, C_BK))[w]
                        act.activation(qkf[:, w, :], bk[:, :], ACT.Identity, bias=col(bias))\
                            .then_inc(S(("qf", "kf")[w]), 1)
                    return step

                def tanh():
                    wait(act, "dlt", g, 1, 1)
                    act.activation(rt[:, 1, :, :], rt[:, 0, :, :], ACT.Tanh, scale=0.5).then_inc(S("th"), 1)

                def w_t():
                    wait(act, "wt", g, 1, 1)
                    wait(act, "w_st", g, 16, 0)
                    act.activation(wT[:, :], b7[0:TT * E, 0:P], ACT.Copy).then_inc(S("wT"), 1)
                return {10: [x_t], 15: [z_t], 17: [tanh], 19: [qk(0)], 21: [qk(1)], 23: [w_t]}

            def experts(g):
                def gelu(i):
                    def step():
                        wait(act, "h", g, HT, i + 1)
                        wait(act, "m2", g, HT, i - 3)
                        e, c = i // HC, i % HC
                        act.activation(hh[:, i % 4, :], bank[i % 2][:, :], ACT.Gelu, bias=col(C_B1 + i))\
                            .then_inc(S("hh"), 1)
                        wait(act, "hl", g, HT, i - 1)
                        act.activation(h32[:, i % 2, :], bank[i % 2][:, :], ACT.Gelu, bias=col(C_B1 + i))\
                            .then_inc(S("h32"), 1)
                    return step
                return {i: [gelu(i)] for i in range(HT)}

            def neg_max_t(it, u, early=False):
                m_tr = (b7 if early else ring_bank("mTc"))[0:PARTS * NT, 0:P // 2].bitcast(BF16)
                wait(act, "mT", it, HB, u + 1)
                wait(act, "m_st", it, HB * 16, (u - 1) * 16)
                act.activation(nmT[:, u % 2, :], m_tr, ACT.Copy).then_inc(S("mTc"), 1)

            def hi(ns):
                return [lambda n=n: weights_hi(n) for n in ns]

            prepare_first(pre, experts, {9: hi(range(2)), 12: hi(range(2, 4)), 18: hi(range(4, RAW))})
            expert_phase(act, experts, pre, first={2 * (n - RAW) + 2: hi([n]) for n in range(RAW, 2 * E)},
                         extra={22: [lambda: (wait(act, "w_st", NG, 16, 0), neg_max_t(0, 0, early=True))]})

            def o_copy(it, u):
                wait(act, "PV", it, HB * KT // 2, (u + 1) * KT // 2)
                wait(act, "ot", it, HB, u - 1)
                act.activation(o_sb[:, u % 2, :], b6[:, :], ACT.Copy).then_inc(S("oe"), 1)

            def att(it, first, last):
                for u in range(HB):
                    for i in range(2 * KT):
                        kt, a = i // 2, i % 2
                        wait(act, "S", it, HB * 2 * KT, u * 2 * KT + i + 1)
                        if i % 4 == 0:
                            wait(act, "PV", it, HB * KT // 2, u * KT // 2 + kt // 2 - 1)
                        act.activation(p_sb[:, kt % 4, a * TG:(a + 1) * TG], ring_bank("P", i)[:, :], ACT.Exp,
                                       scale=SCALE).then_inc(S("P"), 1)
                        if i == 1:
                            if u:
                                o_copy(it, u - 1)
                            elif not first:
                                o_copy(it - 1, HB - 1)
                        if i == 5:
                            if u + 1 < HB:
                                neg_max_t(it, u + 1)
                            elif not last:
                                neg_max_t(it + 1, 0)

            att(0, True, False)
            with act.Fori(1, NIT - 1) as it:
                att(it, False, False)
            att(NIT - 1, False, True)
            o_copy(NIT - 1, HB - 1)

            for g in range(NG):
                act.activation(ffn[:, g, :], ffn[:, g, :], ACT.Silu).then_inc(S("gate"), 1)

        @block.tensor
        def _(pe):
            pe.wait_ge(S("ident"), 2)
            pe.wait_ge(S("rows"), 6 * 16)
            pe.transpose(b7[:, 0:NROW], rows[0:NROW, :], ident[0:NROW, 0:NROW]).then_inc(S("cols_t"), 1)
            pe.wait_ge(S("const"), 4 * 16)

            def pre(g):
                def t1():
                    wait(pe, "xn", g, 1, 1)
                    wait(pe, "qf", g, 1, 0)
                    for t in range(TT):
                        m = pe.transpose(b5[:, t * P:(t + 1) * P], xz[:, t, :], ident[:, :])
                    m.then_inc(S("t1"), 1)

                def t2():
                    wait(pe, "zn", g, 1, 1)
                    wait(pe, "kf", g, 1, 0)
                    for t in range(TT):
                        m = pe.transpose(b6[:, t * P:(t + 1) * P], xz[:, t, :], ident[:, :])
                    m.then_inc(S("t2"), 1)

                def logits():
                    wait(pe, "xnT", g, 1, 1)
                    if isinstance(g, int) and g == 0:
                        pe.wait_ge(S("cols"), 1)
                    wait(pe, "vd", g, 1, 0)
                    for t in range(TT):
                        m = pe.matmul(b7[:, t * E:(t + 1) * E], xnT[:, t * P:(t + 1) * P], wr_sb[:, :],
                                      start=True, stop=True)
                    m.then_inc(S("lg"), 1)

                def qk():
                    wait(pe, "znT", g, 1, 1)
                    pe.matmul(b5[:, :], wqkv_sb[:, 0:D], znT[:, :], start=True, stop=True).then_inc(S("q"), 1)
                    pe.matmul(b6[:, :], wqkv_sb[:, D:2 * D], znT[:, :], start=True, stop=True).then_inc(S("k"), 1)

                def w_t():
                    wait(pe, "w", g, 1, 1)
                    pe.transpose(b7[0:TT * E, 0:P], rt[:, 5, :, :].rearrange("p t e -> p (t e)"), ident[:, :])\
                        .then_inc(S("wt"), 1)

                def v():
                    wait(pe, "wT", g, 1, 1)
                    for t in range(TT):
                        m = pe.matmul(b7[:, t * P:(t + 1) * P], znT[:, t * P:(t + 1) * P], wqkv_sb[:, 2 * D:3 * D],
                                      start=True, stop=True)
                    m.then_inc(S("v"), 1)
                return {9: [t1], 12: [logits], 15: [t2], 18: [qk], 21: [w_t], 25: [v]}

            def experts(g):
                def up(i):
                    def step():
                        if i == 0:
                            wait(pe, "xl", g, 1, 1)
                        if isinstance(g, int) and g == 0 and i % HC == 0:
                            n = 2 * (i // HC) + 2
                            pe.wait_ge(S("w_lo_v" if n <= RAW else "w_lo_p"), n if n <= RAW else n - RAW)
                        wait(pe, "h32", g, HT, i - 1)
                        e, c = i // HC, i % HC
                        o = bank[i % 2][:, :]
                        ws = slice(c * P, (c + 1) * P)
                        pe.matmul(o, w1h[:, e, ws], G(xh, g), start=True, stop=False)
                        pe.matmul(o, w1l[:, e, ws], G(xh, g), start=False, stop=False)
                        pe.matmul(o, w1h[:, e, ws], G(xl, g), start=False, stop=True).then_inc(S("h"), 1)
                    return step

                def down(i):
                    def step():
                        e, c = i // HC, i % HC
                        if c == 0:
                            wait(pe, "stt", g, E, e - 1)
                        o = bank[2 + e % 2][:, :]
                        ws = slice(c * D, (c + 1) * D)
                        wait(pe, "hh", g, HT, i + 1)
                        pe.matmul(o, w2h[:, e, ws], hh[:, i % 4, :], start=(c == 0), stop=False)
                        pe.matmul(o, w2l[:, e, ws], hh[:, i % 4, :], start=False, stop=False)
                        wait(pe, "hl", g, HT, i + 1)
                        pe.matmul(o, w2h[:, e, ws], hl[:, i % 4, :], start=False, stop=(c == HC - 1))\
                            .then_inc(S("m2"), 1)
                    return step
                plan = {i: [up(i)] for i in range(HT)}
                for i in range(HT):
                    plan.setdefault(i + 2, []).append(down(i))
                return plan

            def max_scores(it, u, t, early=False):
                if t == 0:
                    wait(pe, f"st{u}", it, 96, 96)
                if early and (u, t) == (0, 0):
                    pe.wait_ge(S("kf"), NG)
                    pe.wait_ge(S("vd"), NG)
                if early and (u, t) == EARLY_TURN:
                    pe.wait_ge(S("mTc"), 1)
                if isinstance(it, int) and (it, u, t) == (0, 2, 0):
                    pe.wait_ge(S("stt"), NG * E)
                    pe.wait_ge(S("R"), 2 * NT)
                wait(pe, "R", it, HB * NT, u * NT + t - 1)
                first = (4 if early else 2) + 2 * (t % 2)
                for c in range(2):
                    m = pe.matmul(bank[first + c][:, :], q_st[0:QROWS, u, t * P:(t + 1) * P],
                                  k_st[0:QROWS, u, c * TG:(c + 1) * TG], start=True, stop=True)
                m.then_inc(S("M"), 1)

            def ring_free(it, u, what):
                at = RING.index(what) - len(ring)
                n = it * HB + u if isinstance(it, int) else None
                if n is not None:
                    skipped = {("os", 0)} if n == 0 else {("mTc", 0)} if n == NHEAD - 1 else ()
                    while at >= 0 and RING[at] in skipped:
                        at -= len(ring)
                name, i = RING[at]
                u -= at < 0
                if name == "P":
                    wait(pe, "P", it, HB * 2 * KT, u * 2 * KT + i + 1)
                elif name == "mTc":
                    wait(pe, "mTc", it, HB, u + 2)
                else:
                    wait(pe, "os", it, HB, u)

            def m_t(it, u, early=False):
                wait(pe, "nmp", it, HB, u + 1)
                if not early:
                    ring_free(it, u - 1, ("mTc", 0))
                m_tr = (b7 if early else ring_bank("mTc"))[0:PARTS * NT, 0:P // 2].bitcast(BF16)
                pe.transpose(m_tr, nmp[:, u, :, :].rearrange("p i t -> p (i t)"), ident_b[:, :])\
                    .then_inc(S("mT"), 1)

            def early(u, t):
                return lambda: max_scores(0, u, t, early=True)

            beside = {2 * n + 1: [early(n // NT, n % NT)] for n in range(2 * NT)}
            beside[22] = [lambda: (pe.wait_ge(S("R"), NT + 2), m_t(0, 0, early=True))]
            EARLY_TURN = (1, 3)
            prepare_first(pre, experts)
            expert_phase(pe, experts, pre, extra=beside)

            def scores(it, u, i):
                kt, a = i // 2, i % 2
                ring_free(it, u, ("P", i))
                pe.matmul(ring_bank("P", i)[:, :], k_st[0:SROWS, u, kt * P:(kt + 1) * P],
                          q_st[0:SROWS, u, a * TG:(a + 1) * TG], start=True, stop=True).then_inc(S("S"), 1)

            def pv(it, u, m):
                if m == 0:
                    wait(pe, "vst", it, HB, u + 1)
                    wait(pe, "oe", it, HB, u)
                wait(pe, "P", it, HB * 2 * KT, u * 2 * KT + 4 * m + 4)
                for g4 in range(4):
                    kt, a = 2 * m + g4 // 2, g4 % 2
                    mm = pe.matmul(b6[VC * g4:VC * (g4 + 1), :], v_st[:, u, kt, :],
                                   p_sb[:, kt % 4, a * TG:(a + 1) * TG],
                                   start=(m == 0), stop=(m == KT // 2 - 1), skip_group_check=True)
                mm.then_inc(S("PV"), 1)

            def o_t(it, u, final=False):
                wait(pe, "oe", it, HB, u + 1)
                if final:
                    wait(pe, "P", it, HB * 2 * KT, HB * 2 * KT)
                else:
                    ring_free(it, u + 1, ("os", 0))
                for j in range(TT):
                    m = pe.transpose(ring_bank("os")[:, j * P:(j + 1) * P], o_sb[:, u % 2, j * P:(j + 1) * P], ident[:, :])
                m.then_inc(S("ot"), 1)

            def msa_turn(g):
                if g == 0:
                    wait(pe, "R", 0, 0, NHEAD * NT)
                wait(pe, "msa", 0, 0, (g // 2 + 1) * H)
                wait(pe, "tmc", 0, 0, g - 1)
                for t in range(TT):
                    m = pe.transpose(bank[2 + g % 2][:, t * P:(t + 1) * P], msa[:, g * TT + t, :], ident[:, :])
                m.then_inc(S("tm"), 1)

            def project(g):
                if g == 0:
                    pe.wait_ge(S("wp"), 16)
                wait(pe, "tmc", 0, 0, g + 1)
                wait(pe, "y", 0, 0, g - 1)
                pe.matmul(bank[4 + g % 2][:, :], wp_sb[:, :], msaT[:, g % 2, :], start=True, stop=True)\
                    .then_inc(S("tp"), 1)

            def y_turn(g):
                if g in POOL_GATES:
                    wait(pe, "yg_p", 0, 0, POOL_GATES.index(g) + 1)
                else:
                    wait(pe, "yg_v", 0, 0, DVE_GATES.index(g) + 1)
                wait(pe, "ty", 0, 0, g + 1 - len(ring))
                for t in range(TT):
                    m = pe.transpose(ring[g % len(ring)][:, t * P:(t + 1) * P], y[:, g, t * P:(t + 1) * P],
                                     ident[:, :])
                m.then_inc(S("tt"), 1)

            ends = {}
            for g in range(BESIDE):
                ends.setdefault(2 * g, []).append(lambda g=g: msa_turn(g))
                ends.setdefault(2 * g + 2, []).append(lambda g=g: project(g))

            def att(it, first, last):
                for u in range(HB):
                    prev = (it, u - 1) if u else (it - 1, HB - 1)
                    has_prev = not (first and u == 0)
                    wait(pe, f"m_ld{u}", it, 16, 16)
                    for j in range(KT // 2):
                        def heads_max(t):
                            if last and u + 2 >= HB:
                                for step in ends.get((u + 2 - HB) * NT + t, []):
                                    step()
                                return
                            if u + 2 < HB:
                                max_scores(it, u + 2, t)
                            else:
                                max_scores(it + 1, u + 2 - HB, t)
                        scores(it, u, 4 * j)
                        heads_max(2 * j)
                        if j == 2 and has_prev:
                            o_t(*prev)
                        scores(it, u, 4 * j + 1)
                        if j:
                            pv(it, u, j - 1)
                        elif has_prev:
                            pv(*prev, KT // 2 - 1)
                        if j == 1:
                            if u + 1 < HB:
                                m_t(it, u + 1)
                            elif not last:
                                m_t(it + 1, 0)
                        scores(it, u, 4 * j + 2)
                        heads_max(2 * j + 1)
                        scores(it, u, 4 * j + 3)

            pe.wait_ge(S("h32"), NG * HT)
            pe.wait_ge(S("mTc"), 1)
            att(0, True, False)
            with pe.Fori(1, NIT - 1) as it:
                att(it, False, False)
            att(NIT - 1, False, True)
            pv(NIT - 1, HB - 1, KT // 2 - 1)
            o_t(NIT - 1, HB - 1, final=True)

            for step in (msa_turn, project, y_turn):
                for g in range(0 if step is y_turn else BESIDE, NG):
                    step(g)

        @block.vector
        def _(dve):
            ch = Chain(dve, S("dve_own"))

            def guess_rsqrt(g, k):
                def step():
                    v, y, hv = (nwt[:, i, :] for i in range(3))
                    ch.mark(dve.tensor_scalar(v, mv[:, :, 1], EPS, None, ALU.add))
                    ch.sync()
                    ch.mark(dve.tensor_scalar(guess[:, :], v.bitcast(I32), 1, None, ALU.logical_shift_right))
                    ch.mark(dve.tensor_scalar(hv, v, -0.5, None, ALU.mult))
                    ch.sync()
                    dve.tensor_scalar(y.bitcast(I32), guess[:, :], -1.0, float(RSQRT_GUESS), ALU.mult, ALU.add)\
                        .then_inc(S("guess"), 1)
                    if isinstance(g, int) and g == 0:
                        newton(k)
                return step

            def newton(k):
                y, hv, a = (nwt[:, i, :] for i in (1, 2, 3))
                dve.wait_ge(S("guess"), k)
                for n in range(NEWTON):
                    ch.mark(dve.tensor_tensor(a, y, y, ALU.mult))
                    ch.sync()
                    ch.mark(dve.tensor_tensor(a, a, hv, ALU.mult))
                    ch.sync()
                    i = dve.scalar_tensor_tensor(y, a, 1.5, y, ALU.add, ALU.mult)
                    if n < NEWTON - 1:
                        ch.mark(i)
                        ch.sync()
                i.then_inc(S("nwt"), 1)

            def spread(t0, t1):
                def step():
                    for t in range(t0, t1):
                        i = dve.bn_stats(st1[:, t, :], xz[:, t, :])
                    ch.mark(i)
                return step

            def moments():
                ch.sync()
                for t in range(TT):
                    i = dve.bn_aggr(mv[:, t, :], st1[:, t, :])
                ch.mark(i)
                ch.sync()

            def pre(g):
                def x_here():
                    wait(dve, "x", g, 16, 16)

                def z_here():
                    wait(dve, "xn", g, 1, 1)

                def normalise(done):
                    def step():
                        wait(dve, "nwt", g, 2, 1 if done == "xn" else 2)
                        if done == "zn":
                            wait(dve, "t1", g, 1, 1)
                        for t in range(TT):
                            i = dve.tensor_scalar(xz[:, t, :], xz[:, t, :], mv[:, t, 0:1], nwt[:, 1, t:t + 1],
                                                  ALU.subtract, ALU.mult)
                        i.then_inc(S(done), 1)
                    return step

                def high_x():
                    wait(dve, "xnT", g, 1, 1)
                    dve.tensor_copy(G(xh, g), xnT[:, :]).then_inc(S("xh"), 1)

                def low_x():
                    wait(dve, "xh", g, 1, 1)
                    dve.tensor_tensor(G(xl, g), xnT[:, :], G(xh, g).bitcast(F32), ALU.subtract)\
                        .then_inc(S("xl"), 1)

                def router_top():
                    wait(dve, "lg", g, 1, 1)
                    ch.mark(dve.tensor_tensor(lg[:, :, :], b7[:, 0:TT * E].rearrange("p (t e) -> p t e", e=E),
                                              br_bc[:, :].unsqueeze(1).broadcast_to([P, TT, E]), ALU.add))
                    ch.sync()
                    for t in range(TT):
                        i = dve.max(top[:, t, :], lg[:, t, :])
                    ch.mark(i)
                    ch.sync()
                    dve.tensor_tensor(rt[:, 0, :, :], lg[:, :, :], top[:, :, 0:1].broadcast_to([P, TT, E]),
                                      ALU.subtract).then_inc(S("dlt"), 1)
                    ch.mark(dve.tensor_tensor(rt[:, 2, :, :], lg[:, :, :], top[:, :, 1:2].broadcast_to([P, TT, E]),
                                              ALU.is_ge))

                def router_weights():
                    wait(dve, "th", g, 1, 1)
                    ch.mark(dve.tensor_scalar(rt[:, 3, :, :], rt[:, 1, :, :], 1.0, None, ALU.add))
                    ch.mark(dve.tensor_scalar(rt[:, 4, :, :], rt[:, 1, :, :], -1.0, 1.0, ALU.mult, ALU.add))
                    ch.sync()
                    ch.mark(dve.reciprocal(rt[:, 4, :, :], rt[:, 4, :, :]))
                    ch.sync()
                    ch.mark(dve.tensor_tensor(rt[:, 3, :, :], rt[:, 3, :, :], rt[:, 4, :, :], ALU.mult))

                def router_sum():
                    ch.sync()
                    ch.mark(dve.tensor_tensor(rt[:, 3, :, :], rt[:, 3, :, :], rt[:, 2, :, :], ALU.mult))
                    ch.sync()
                    ch.mark(dve.tensor_reduce(rs[:, 0, :], rt[:, 3, :, :], AX.X, ALU.add))
                    ch.sync()
                    ch.mark(dve.reciprocal(rs[:, 1, :], rs[:, 0, :]))

                def router_done():
                    ch.end()
                    wait(dve, "wt", g, 1, 0)
                    dve.tensor_tensor(rt[:, 5, :, :], rt[:, 3, :, :],
                                      rs[:, 1, :].unsqueeze(2).broadcast_to([P, TT, E]), ALU.mult)\
                        .then_inc(S("w"), 1)

                def first(w):
                    def step():
                        wait(dve, ("qf", "kf")[w], g, 1, 1)
                        wait(dve, "qp_st", g, QP_ST, 0)
                        dve.tensor_copy(qkp[:, w, 0, :], qkf[:, w, :]).then_inc(S("p0"), 1)
                    return step

                def second(w):
                    def step():
                        wait(dve, "r1", g, 2, w + 1)
                        dve.tensor_copy(qkp[:, w, 1, :], qkf[:, w, :]).then_inc(S("p1"), 1)
                    return step

                def values():
                    wait(dve, "v", g, 1, 1)
                    dst = v_sb[:, g * TT:(g + 1) * TT, :] if isinstance(g, int) else v_sb[:, bass.ds(g * TT, TT), :]
                    dve.tensor_tensor(dst, b7[:, :].rearrange("p (t d) -> p t d", d=D),
                                      bv_bc[:, :].unsqueeze(1).broadcast_to([P, TT, D]), ALU.add)\
                        .then_inc(S("vd"), 1)
                return {0: [x_here, spread(0, 1)], 1: [spread(1, 4)], 3: [moments, guess_rsqrt(g, 1)],
                        7: [normalise("xn")], 8: [z_here, spread(0, 4)], 9: [moments, guess_rsqrt(g, 2)],
                        11: [high_x], 12: [low_x], 13: [normalise("zn")], 15: [router_top],
                        17: [router_weights], 18: [router_sum], 19: [router_done],
                        20: [first(0)], 21: [first(1)], 24: [second(0)], 25: [second(1)], 28: [values]}

            def experts(g):
                def low_h(i):
                    def step():
                        wait(dve, "h32", g, HT, i + 1)
                        wait(dve, "m2", g, HT, i - 3)
                        dve.tensor_tensor(hl[:, i % 4, :], h32[:, i % 2, :], hh[:, i % 4, :].bitcast(F32),
                                          ALU.subtract).then_inc(S("hl"), 1)
                    return step

                def combine(e):
                    def step():
                        wait(dve, "m2", g, HT, (e + 1) * HC)
                        if isinstance(g, int):
                            dve.wait_ge(s_wbc[e], 16 * (g + 1))
                        else:
                            dve.wait_ge(s_wbc[e], 16 * g + 16)
                        if e == 0:
                            wait(dve, "acc", g, E - 1, 0)
                        if e > 2:
                            wait(dve, "acc", g, E - 1, e - 2)
                        dst = prod[:, e % 2, :] if e else acc[:, :]
                        dve.scalar_tensor_tensor(dst, bank[2 + e % 2][:, :], col(C_B2 + e), wbc[:, e, :],
                                                 ALU.add, ALU.mult).then_inc(S("stt"), 1)
                    return step
                def total():
                    wait(dve, "stt", g, E, E)
                    wait(dve, "acc", g, E - 1, E - 2)
                    dve.tensor_tensor(G(ffn, g), acc[:, :], prod[:, (E - 1) % 2, :], ALU.add).then_inc(S("acc"), 1)

                plan = {4 * e + 6: [combine(e)] for e in range(E)}
                plan[4 * E + 4] = [total]
                for i in range(HT):
                    plan.setdefault(i, []).append(low_h(i))
                return plan

            def row_max(it, u, t, early=False):
                wait(dve, "M", it, HB * NT, u * NT + t + 1)
                pair = psum[:, (4 + 2 * (t % 2)) * TG:(6 + 2 * (t % 2)) * TG] if early else wide_banks[t % 2]
                dve.tensor_reduce(mx[:, u, t:t + 1], pair, AX.X, ALU.max, negate=True).then_inc(S("R"), 1)

            def lo(ns):
                return [lambda n=n: weights_lo(dve, n) for n in ns]

            def early(u, t):
                return lambda: row_max(0, u, t, early=True)

            prepare_first(pre, experts, {12: lo(range(2)), 14: lo([2]), 17: lo([3]), 21: lo(range(4, RAW))}, AHEAD_V)
            expert_phase(dve, experts, pre, extra={2 * n + 2: [early(n // NT, n % NT)] for n in range(2 * NT)})

            def head_out(it, u):
                wait(dve, "ot", it, HB, u + 1)
                turned = ring_bank("os")[:, :].rearrange("p (j k a r) -> p a j r k", k=2, a=2, r=VC)
                for a in range(2):
                    i = dve.tensor_reduce(o9[:, u % 2, a * TT:(a + 1) * TT, :], turned[:, a, :, 0:DH + 1, :],
                                          AX.X, ALU.add)
                i.then_inc(S("os"), 1)
                wait(dve, "os", it, HB, u + 1)
                dve.reciprocal(rden[:, u % 2, :], o9[:, u % 2, :, DH]).then_inc(S("rd"), 1)
                wait(dve, "rd", it, HB, u + 1)
                b, h = it // (H // HB), (it % (H // HB)) * HB + u
                dst = msa[:, b * NT:(b + 1) * NT, h * DH:(h + 1) * DH] if isinstance(it, int) else \
                    msa[:, bass.ds(b * NT, NT), bass.ds(h * DH, DH)]
                dve.tensor_tensor(dst, o9[:, u % 2, :, 0:DH], rden[:, u % 2, :].unsqueeze(2)
                                  .broadcast_to([P, NT, DH]), ALU.mult).then_inc(S("msa"), 1)

            def msa_copy(g):
                wait(dve, "tm", 0, 0, g + 1)
                wait(dve, "tp", 0, 0, g - 1)
                dve.tensor_copy(msaT[:, g % 2, :], bank[2 + g % 2][:, :]).then_inc(S("tmc"), 1)

            def sum_y(g):
                wait(dve, "tp", 0, 0, g + 1)
                wait(dve, "xf", 0, 0, g + 1)
                dve.scalar_tensor_tensor(y[:, g, :], bank[4 + g % 2][:, :], col(C_BP), y[:, g, :],
                                         ALU.add, ALU.add).then_inc(S("y"), 1)

            def gate_y(g):
                wait(dve, "gate", 0, 0, g + 1)
                wait(dve, "y", 0, 0, g + 1)
                dve.tensor_tensor(y[:, g, :], y[:, g, :], ffn[:, g, :], ALU.mult).then_inc(S("yg_v"), 1)

            def finish(g):
                if g == 0:
                    wait(dve, "tx", 0, 0, 16 * NG)
                wait(dve, "tt", 0, 0, g + 1)
                dst = x_out[:, g, :, :]
                dve.tensor_tensor(dst, ring[g % len(ring)][:, :].rearrange("p (t d) -> p t d", d=D), dst, ALU.add)\
                    .then_inc(S("ty"), 1)

            ends = {}
            for g in range(BESIDE):
                ends.setdefault(2 * g, []).append(lambda g=g: msa_copy(g))
                ends.setdefault(2 * g + 2, []).append(lambda g=g: sum_y(g))

            def att(it, first, last):
                for u in range(HB):
                    for t in range(NT):
                        m = u + 2
                        if m < HB:
                            row_max(it, m, t)
                        elif not last:
                            row_max(it + 1, m - HB, t)
                        if t == 4 and not (first and u == 0):
                            head_out(*((it, u - 1) if u else (it - 1, HB - 1)))
                        if last and m >= HB:
                            for step in ends.get((m - HB) * NT + t, []):
                                step()

            att(0, True, False)
            with dve.Fori(1, NIT - 1) as it:
                att(it, False, False)
            att(NIT - 1, False, True)
            head_out(NIT - 1, HB - 1)
            for g in range(BESIDE, NG):
                msa_copy(g)
            for g in range(BESIDE, NG):
                sum_y(g)
            for g in range(NG):
                if g in DVE_GATES:
                    gate_y(g)
                if g:
                    finish(g - 1)
            finish(NG - 1)


_INS = ["L0_attn_z", "L0_attn_ln_w", "L0_attn_ln_b", "L0_attn_W_qkv", "L0_attn_b_qkv", "L0_attn_W_proj",
        "L0_attn_b_proj", "L0_ffn_W1", "L0_ffn_b1", "L0_ffn_W2", "L0_ffn_b2", "L0_ffn_Wr", "L0_ffn_br"]


def kernel(**inputs):
    import numpy as _np
    import concourse.bacc as _bacc
    from concourse import mybir as _mybir
    from concourse.bass_utils import run_bass_kernel_spmd as _run

    nc = _bacc.Bacc("TRN2", target_bir_lowering=False, num_devices=1)
    arrays, args = {}, []
    for name in _INS:
        a = _np.ascontiguousarray(inputs[name])
        arrays[f"in_{name}_dram"] = a
        args.append(nc.dram_tensor(f"in_{name}_dram", a.shape, _mybir.dt.from_np(a.dtype), kind="ExternalInput").ap())
    shape = inputs["L0_attn_z"].shape
    args.append(nc.dram_tensor("out_0_dram", shape, _mybir.dt.float32, kind="ExternalOutput").ap())
    attention_and_experts(nc, *args)
    r = _run(nc, [arrays], core_ids=[0])
    return r.results[0]["out_0_dram"]
```
